# Optimizing a Trainium2 kernel written in Bass

```python
import numpy as np
import jax
import jax.numpy as jnp

def _softmax(x, axis=-1):
    return jax.nn.softmax(x, axis=axis)

def _gelu(x):
    return jax.nn.gelu(x, approximate=True)

def _silu(x):
    return jax.nn.silu(x)

def _sigmoid(x):
    return jax.nn.sigmoid(x)

def _layernorm(x, axis=-1, eps=1e-05):
    m = jnp.mean(x, axis=axis, keepdims=True)
    v = jnp.var(x, axis=axis, keepdims=True)
    return (x - m) / jnp.sqrt(v + eps)

def _scatter_add(tgt, idx, src, axis=0):
    return tgt.at[idx].add(src)

def _segment_sum(src, seg, n):
    return jax.ops.segment_sum(src, seg, n)
kernel_name = 'mk_conv_attn_hybrid_d4_conv_nhwc256_r4_5ef033'

def setup_inputs(seed: int=0):
    np.random.seed(seed)
    _w = jnp.asarray

    def _rec_inputs():
        import jax
        import jax.numpy as jnp
        _gk = jax.random.key(seed)
        x = -0.0005207 + 1.001 * jax.random.normal(jax.random.fold_in(_gk, 1), (2, 16, 16, 64), jnp.float32)
        return x
    x = _rec_inputs()

    def _L0_conv_setup():
        import jax, jax.numpy as jnp
        import numpy as np
        B, N, D, H = (2, 16, 64, 8)
        DK = D // H
        EPS = 1e-05

        def layer_norm(x, g, b):
            mu = jnp.mean(x, axis=-1, keepdims=True)
            var = jnp.var(x, axis=-1, keepdims=True)
            return (x - mu) * jax.lax.rsqrt(var + EPS) * g + b
        key = jax.random.key(seed)
        ks = jax.random.split(key, 12)
        s = 1.0 / np.sqrt(D)
        inp = {'x': jax.random.normal(ks[0], (B, N, N, D), jnp.float32), 'W_lk': jax.random.uniform(ks[1], (D, D), jnp.float32, -s, s), 'W_rk': jax.random.uniform(ks[2], (D, D), jnp.float32, -s, s), 'W_lv': jax.random.uniform(ks[3], (D, D), jnp.float32, -s, s), 'W_rv': jax.random.uniform(ks[4], (D, D), jnp.float32, -s, s), 'W_out': jax.random.uniform(ks[5], (D, D), jnp.float32, -s, s), 'ln_agg_g': jnp.ones((D,), jnp.float32), 'ln_agg_b': jnp.zeros((D,), jnp.float32), 'W1': jax.random.uniform(ks[6], (D, 2 * D), jnp.float32, -s, s), 'b1': jnp.zeros((2 * D,), jnp.float32), 'W2': jax.random.uniform(ks[7], (2 * D, D), jnp.float32, -1.0 / np.sqrt(2 * D), 1.0 / np.sqrt(2 * D)), 'b2': jnp.zeros((D,), jnp.float32), 'ln2_g': jnp.ones((D,), jnp.float32), 'ln2_b': jnp.zeros((D,), jnp.float32)}
        return inp
    _L0_conv_all = _L0_conv_setup()
    _L0_conv_in = {k: v for k, v in _L0_conv_all.items() if k in ('W_lk', 'W_rk', 'W_lv', 'W_rv', 'W_out', 'ln_agg_g', 'ln_agg_b', 'W1', 'b1', 'W2', 'b2', 'ln2_g', 'ln2_b')}
    del _L0_conv_all

    def _L1_conv_setup():
        import jax, jax.numpy as jnp
        import numpy as np
        ROPE_BASE = 10000.0

        def _rope_cos_sin(n, d, dtype):
            inv_freq = 1.0 / ROPE_BASE ** (jnp.arange(0, d, 2, dtype=jnp.float32) / d)
            ang = jnp.arange(n, dtype=jnp.float32)[:, None] * inv_freq[None, :]
            return (jnp.cos(ang).astype(dtype), jnp.sin(ang).astype(dtype))

        def _apply_rope(t, cos, sin):
            d2 = t.shape[-1] // 2
            t1, t2 = (t[..., :d2], t[..., d2:])
            return jnp.concatenate([t1 * cos - t2 * sin, t2 * cos + t1 * sin], axis=-1)
        key = jax.random.key(seed)
        ks = jax.random.split(key, 8)
        B, H, W, C = (4, 48, 48, 64)
        s = 1.0 / np.sqrt(C)
        return {'x': jax.random.normal(ks[0], (B, H, W, C), dtype=jnp.float32), 'Wq': jax.random.normal(ks[1], (C, C), dtype=jnp.float32) * s, 'q_bias': jax.random.normal(ks[2], (C,), dtype=jnp.float32) * 0.02, 'Wk': jax.random.normal(ks[3], (C, C), dtype=jnp.float32) * s, 'Wv': jax.random.normal(ks[4], (C, C), dtype=jnp.float32) * s, 'v_bias': jax.random.normal(ks[5], (C,), dtype=jnp.float32) * 0.02, 'Wo': jax.random.normal(ks[6], (C, C), dtype=jnp.float32) * s, 'bo': jax.random.normal(ks[7], (C,), dtype=jnp.float32) * 0.02}
    _L1_conv_all = _L1_conv_setup()
    _L1_conv_in = {k: v for k, v in _L1_conv_all.items() if k in ('Wq', 'q_bias', 'Wk', 'Wv', 'v_bias', 'Wo', 'bo')}
    del _L1_conv_all

    def _L2_attn_setup():
        import jax, jax.numpy as jnp
        import numpy as np
        key = jax.random.key(seed)
        ks = jax.random.split(key, 6)
        b, t, k, h = (2, 512, 64, 8)
        s = 1.0 / np.sqrt(k)
        return {'x': jax.random.normal(ks[0], (b, t, k), dtype=jnp.float32), 'Wq': jax.random.normal(ks[1], (k, k * h), dtype=jnp.float32) * s, 'Wk': jax.random.normal(ks[2], (k, k * h), dtype=jnp.float32) * s, 'Wv': jax.random.normal(ks[3], (k, k * h), dtype=jnp.float32) * s, 'Wu': jax.random.normal(ks[4], (k * h, k), dtype=jnp.float32) * (1.0 / np.sqrt(k * h)), 'bu': jnp.zeros((k,), dtype=jnp.float32)}
    _L2_attn_all = _L2_attn_setup()
    _L2_attn_in = {k: v for k, v in _L2_attn_all.items() if k in ('Wq', 'Wk', 'Wv', 'Wu', 'bu')}
    del _L2_attn_all

    def _L2_ffn_setup():
        import jax, jax.numpy as jnp
        import numpy as np
        TOP_K = 2
        LN_EPS = 1e-05
        key = jax.random.key(seed)
        ks = jax.random.split(key, 8)
        B, S, D, E, H = (16, 256, 64, 8, 256)
        x = jax.random.normal(ks[0], (B, S, D), dtype=jnp.float32)
        Wr = jax.random.normal(ks[1], (D, E), dtype=jnp.float32) * 0.1
        br = jnp.zeros((E,), dtype=jnp.float32)
        ln_g = jnp.ones((E, D), dtype=jnp.float32)
        ln_b = jnp.zeros((E, D), dtype=jnp.float32)
        W1 = jax.random.normal(ks[2], (E, D, H), dtype=jnp.float32) * (1.0 / np.sqrt(D))
        b1 = jnp.zeros((E, H), dtype=jnp.float32)
        W2 = jax.random.normal(ks[3], (E, H, D), dtype=jnp.float32) * (1.0 / np.sqrt(H))
        b2 = jnp.zeros((E, D), dtype=jnp.float32)
        return {'x': x, 'Wr': Wr, 'br': br, 'ln_g': ln_g, 'ln_b': ln_b, 'W1': W1, 'b1': b1, 'W2': W2, 'b2': b2}
    _L2_ffn_all = _L2_ffn_setup()
    _L2_ffn_in = {k: v for k, v in _L2_ffn_all.items() if k in ('Wr', 'br', 'ln_g', 'ln_b', 'W1', 'b1', 'W2', 'b2')}
    del _L2_ffn_all

    def _L3_attn_setup():
        import jax, jax.numpy as jnp
        import numpy as np
        D_STATE = 16
        D_CONV = 4
        DT_RANK = 16
        EPS = 1e-05

        def rmsnorm(x, w):
            return x * jax.lax.rsqrt(jnp.mean(x * x, axis=-1, keepdims=True) + EPS) * w

        def selective_scan(u, dt, A, Bm, Cm, Dp):

            def step(h, inp):
                u_t, dt_t, B_t, C_t = inp
                h = jnp.exp(dt_t[..., None] * A) * h + (dt_t * u_t)[..., None] * B_t[:, None, :]
                y_t = jnp.einsum('bds,bs->bd', h, C_t)
                return (h, y_t)
            Bsz, L, dI = u.shape
            h0 = jnp.zeros((Bsz, dI, D_STATE), u.dtype)
            xs = (u.transpose(1, 0, 2), dt.transpose(1, 0, 2), Bm.transpose(1, 0, 2), Cm.transpose(1, 0, 2))
            _, ys = jax.lax.scan(step, h0, xs)
            return ys.transpose(1, 0, 2) + u * Dp

        def mamba_mixer(x, in_w, cw, cb, xp_w, dt_w, dt_b, A_log, Dp, out_w):
            xz = x @ in_w
            u, z = jnp.split(xz, 2, axis=-1)
            dI = u.shape[-1]
            uc = jax.lax.conv_general_dilated(u.transpose(0, 2, 1), cw[:, None, :], window_strides=(1,), padding=[(D_CONV - 1, 0)], dimension_numbers=('NCH', 'OIH', 'NCH'), feature_group_count=dI)
            uc = jax.nn.silu(uc.transpose(0, 2, 1) + cb)
            x_dbl = uc @ xp_w
            dt_r = x_dbl[..., :DT_RANK]
            Bm = x_dbl[..., DT_RANK:DT_RANK + D_STATE]
            Cm = x_dbl[..., DT_RANK + D_STATE:]
            dt = jax.nn.softplus(dt_r @ dt_w + dt_b)
            A = -jnp.exp(A_log)
            y = selective_scan(uc, dt, A, Bm, Cm, Dp)
            y = y * jax.nn.silu(z)
            return y @ out_w
        key = jax.random.key(seed)
        n_layer, d, dI = (6, 64, 128)
        B, L = (16, 256)
        ks = jax.random.split(key, 8)
        x = jax.random.normal(ks[0], (B, L, d), jnp.float32)
        in_proj_w = 0.02 * jax.random.normal(ks[1], (n_layer, d, 2 * dI), jnp.float32)
        conv_w = 0.2 * jax.random.normal(ks[2], (n_layer, dI, D_CONV), jnp.float32)
        conv_b = jnp.zeros((n_layer, dI), jnp.float32)
        x_proj_w = 0.02 * jax.random.normal(ks[3], (n_layer, dI, DT_RANK + 2 * D_STATE), jnp.float32)
        dt_proj_w = DT_RANK ** (-0.5) * jax.random.normal(ks[4], (n_layer, DT_RANK, dI), jnp.float32)
        dt_init = jnp.exp(jax.random.uniform(ks[5], (n_layer, dI), jnp.float32) * (np.log(0.1) - np.log(0.001)) + np.log(0.001))
        dt_proj_b = dt_init + jnp.log(-jnp.expm1(-dt_init))
        A_log = jnp.log(jnp.broadcast_to(jnp.arange(1, D_STATE + 1, dtype=jnp.float32), (n_layer, dI, D_STATE)))
        D = jnp.ones((n_layer, dI), jnp.float32)
        out_proj_w = 0.02 * jax.random.normal(ks[6], (n_layer, dI, d), jnp.float32)
        norm_w = jnp.ones((n_layer, d), jnp.float32)
        norm_f_w = jnp.ones((d,), jnp.float32)
        return {'x': x, 'norm_w': norm_w, 'in_proj_w': in_proj_w, 'conv_w': conv_w, 'conv_b': conv_b, 'x_proj_w': x_proj_w, 'dt_proj_w': dt_proj_w, 'dt_proj_b': dt_proj_b, 'A_log': A_log, 'D': D, 'out_proj_w': out_proj_w, 'norm_f_w': norm_f_w}
    _L3_attn_all = _L3_attn_setup()
    _L3_attn_in = {k: v for k, v in _L3_attn_all.items() if k in ('norm_w', 'in_proj_w', 'conv_w', 'conv_b', 'x_proj_w', 'dt_proj_w', 'dt_proj_b', 'A_log', 'D', 'out_proj_w', 'norm_f_w')}
    del _L3_attn_all

    def _L3_ffn_setup():
        import math
        import jax, jax.numpy as jnp
        import numpy as np
        CAPACITY_FACTOR = 1.25
        TOP_K = 2
        LN_EPS = 1e-05

        def _layer_norm(x, gamma, beta):
            mu = jnp.mean(x, axis=-1, keepdims=True)
            var = jnp.var(x, axis=-1, keepdims=True)
            return (x - mu) * jax.lax.rsqrt(var + LN_EPS) * gamma + beta
        key = jax.random.key(seed)
        ks = jax.random.split(key, 4)
        B, S, D, F, E = (8, 1024, 64, 128, 8)
        x = jax.random.normal(ks[0], (B, S, D), dtype=jnp.float32)
        Wr = jax.random.normal(ks[1], (D, E), dtype=jnp.float32) / np.sqrt(D)
        br = jnp.zeros((E,), jnp.float32)
        W1 = jax.random.normal(ks[2], (E, D, F), dtype=jnp.float32) / np.sqrt(D)
        b1 = jnp.zeros((E, F), jnp.float32)
        W2 = jax.random.normal(ks[3], (E, F, D), dtype=jnp.float32) / np.sqrt(F)
        b2 = jnp.zeros((E, D), jnp.float32)
        gamma = jnp.ones((D,), jnp.float32)
        beta = jnp.zeros((D,), jnp.float32)
        return {'x': x, 'Wr': Wr, 'br': br, 'W1': W1, 'b1': b1, 'W2': W2, 'b2': b2, 'gamma': gamma, 'beta': beta}
    _L3_ffn_all = _L3_ffn_setup()
    _L3_ffn_in = {k: v for k, v in _L3_ffn_all.items() if k in ('Wr', 'br', 'W1', 'b1', 'W2', 'b2', 'gamma', 'beta')}
    del _L3_ffn_all
    return {'x': x, 'L0_conv_W_lk': _L0_conv_in['W_lk'], 'L0_conv_W_rk': _L0_conv_in['W_rk'], 'L0_conv_W_lv': _L0_conv_in['W_lv'], 'L0_conv_W_rv': _L0_conv_in['W_rv'], 'L0_conv_W_out': _L0_conv_in['W_out'], 'L0_conv_ln_agg_g': _L0_conv_in['ln_agg_g'], 'L0_conv_ln_agg_b': _L0_conv_in['ln_agg_b'], 'L0_conv_W1': _L0_conv_in['W1'], 'L0_conv_b1': _L0_conv_in['b1'], 'L0_conv_W2': _L0_conv_in['W2'], 'L0_conv_b2': _L0_conv_in['b2'], 'L0_conv_ln2_g': _L0_conv_in['ln2_g'], 'L0_conv_ln2_b': _L0_conv_in['ln2_b'], 'L1_conv_Wq': _L1_conv_in['Wq'], 'L1_conv_q_bias': _L1_conv_in['q_bias'], 'L1_conv_Wk': _L1_conv_in['Wk'], 'L1_conv_Wv': _L1_conv_in['Wv'], 'L1_conv_v_bias': _L1_conv_in['v_bias'], 'L1_conv_Wo': _L1_conv_in['Wo'], 'L1_conv_bo': _L1_conv_in['bo'], 'L2_attn_Wq': _L2_attn_in['Wq'], 'L2_attn_Wk': _L2_attn_in['Wk'], 'L2_attn_Wv': _L2_attn_in['Wv'], 'L2_attn_Wu': _L2_attn_in['Wu'], 'L2_attn_bu': _L2_attn_in['bu'], 'L2_ffn_Wr': _L2_ffn_in['Wr'], 'L2_ffn_br': _L2_ffn_in['br'], 'L2_ffn_ln_g': _L2_ffn_in['ln_g'], 'L2_ffn_ln_b': _L2_ffn_in['ln_b'], 'L2_ffn_W1': _L2_ffn_in['W1'], 'L2_ffn_b1': _L2_ffn_in['b1'], 'L2_ffn_W2': _L2_ffn_in['W2'], 'L2_ffn_b2': _L2_ffn_in['b2'], 'L3_attn_norm_w': _L3_attn_in['norm_w'], 'L3_attn_in_proj_w': _L3_attn_in['in_proj_w'], 'L3_attn_conv_w': _L3_attn_in['conv_w'], 'L3_attn_conv_b': _L3_attn_in['conv_b'], 'L3_attn_x_proj_w': _L3_attn_in['x_proj_w'], 'L3_attn_dt_proj_w': _L3_attn_in['dt_proj_w'], 'L3_attn_dt_proj_b': _L3_attn_in['dt_proj_b'], 'L3_attn_A_log': _L3_attn_in['A_log'], 'L3_attn_D': _L3_attn_in['D'], 'L3_attn_out_proj_w': _L3_attn_in['out_proj_w'], 'L3_attn_norm_f_w': _L3_attn_in['norm_f_w'], 'L3_ffn_Wr': _L3_ffn_in['Wr'], 'L3_ffn_br': _L3_ffn_in['br'], 'L3_ffn_W1': _L3_ffn_in['W1'], 'L3_ffn_b1': _L3_ffn_in['b1'], 'L3_ffn_W2': _L3_ffn_in['W2'], 'L3_ffn_b2': _L3_ffn_in['b2'], 'L3_ffn_gamma': _L3_ffn_in['gamma'], 'L3_ffn_beta': _L3_ffn_in['beta']}

def reference(x, L0_conv_W_lk, L0_conv_W_rk, L0_conv_W_lv, L0_conv_W_rv, L0_conv_W_out, L0_conv_ln_agg_g, L0_conv_ln_agg_b, L0_conv_W1, L0_conv_b1, L0_conv_W2, L0_conv_b2, L0_conv_ln2_g, L0_conv_ln2_b, L1_conv_Wq, L1_conv_q_bias, L1_conv_Wk, L1_conv_Wv, L1_conv_v_bias, L1_conv_Wo, L1_conv_bo, L2_attn_Wq, L2_attn_Wk, L2_attn_Wv, L2_attn_Wu, L2_attn_bu, L2_ffn_Wr, L2_ffn_br, L2_ffn_ln_g, L2_ffn_ln_b, L2_ffn_W1, L2_ffn_b1, L2_ffn_W2, L2_ffn_b2, L3_attn_norm_w, L3_attn_in_proj_w, L3_attn_conv_w, L3_attn_conv_b, L3_attn_x_proj_w, L3_attn_dt_proj_w, L3_attn_dt_proj_b, L3_attn_A_log, L3_attn_D, L3_attn_out_proj_w, L3_attn_norm_f_w, L3_ffn_Wr, L3_ffn_br, L3_ffn_W1, L3_ffn_b1, L3_ffn_W2, L3_ffn_b2, L3_ffn_gamma, L3_ffn_beta):
    import jax
    import jax.numpy as jnp

    def _L0_conv_ref(x, W_lk, W_rk, W_lv, W_rv, W_out, ln_agg_g, ln_agg_b, W1, b1, W2, b2, ln2_g, ln2_b):
        import jax, jax.numpy as jnp
        import numpy as np
        B, N, D, H = (2, 16, 64, 8)
        DK = D // H
        EPS = 1e-05

        def layer_norm(x, g, b):
            mu = jnp.mean(x, axis=-1, keepdims=True)
            var = jnp.var(x, axis=-1, keepdims=True)
            return (x - mu) * jax.lax.rsqrt(var + EPS) * g + b
        b, n = (x.shape[0], x.shape[1])
        lk = (x @ W_lk).reshape(b, n, n, H, DK)
        rk = (x @ W_rk).reshape(b, n, n, H, DK)
        lv = (x @ W_lv).reshape(b, n, n, H, DK)
        rv = (x @ W_rv).reshape(b, n, n, H, DK)
        scores = jnp.einsum('bxahd,bayhd->bxayh', lk, rk) / np.sqrt(DK)
        att = jax.nn.softmax(scores, axis=2)
        o = jnp.einsum('bxayh,bxahd,bayhd->bxyhd', att, lv, rv)
        o = o.reshape(b, n, n, D) @ W_out
        h = layer_norm(x + o, ln_agg_g, ln_agg_b)
        m = jax.nn.relu(h @ W1 + b1) @ W2 + b2
        return layer_norm(m + h, ln2_g, ln2_b)

    def _L1_conv_ref(x, Wq, q_bias, Wk, Wv, v_bias, Wo, bo):
        import jax, jax.numpy as jnp
        import numpy as np
        ROPE_BASE = 10000.0

        def _rope_cos_sin(n, d, dtype):
            inv_freq = 1.0 / ROPE_BASE ** (jnp.arange(0, d, 2, dtype=jnp.float32) / d)
            ang = jnp.arange(n, dtype=jnp.float32)[:, None] * inv_freq[None, :]
            return (jnp.cos(ang).astype(dtype), jnp.sin(ang).astype(dtype))

        def _apply_rope(t, cos, sin):
            d2 = t.shape[-1] // 2
            t1, t2 = (t[..., :d2], t[..., d2:])
            return jnp.concatenate([t1 * cos - t2 * sin, t2 * cos + t1 * sin], axis=-1)
        B, H, W, C = x.shape
        num_heads = 8
        head_dim = C // num_heads
        N = H * W
        xf = x.reshape(B, N, C)
        q = xf @ Wq.T + q_bias
        k = xf @ Wk.T
        v = xf @ Wv.T + v_bias
        q = q.reshape(B, N, num_heads, head_dim).transpose(0, 2, 1, 3)
        k = k.reshape(B, N, num_heads, head_dim).transpose(0, 2, 1, 3)
        v = v.reshape(B, N, num_heads, head_dim).transpose(0, 2, 1, 3)
        cos, sin = _rope_cos_sin(N, head_dim, q.dtype)
        q = _apply_rope(q, cos, sin)
        k = _apply_rope(k, cos, sin)
        scale = head_dim ** (-0.5)
        scores = jnp.einsum('bhnd,bhmd->bhnm', q, k) * scale
        attn = jax.nn.softmax(scores, axis=-1)
        out = jnp.einsum('bhnm,bhmd->bhnd', attn, v)
        out = out.transpose(0, 2, 1, 3).reshape(B, H, W, C)
        return out @ Wo.T + bo

    def _L2_attn_ref(x, Wq, Wk, Wv, Wu, bu):
        import jax, jax.numpy as jnp
        import numpy as np
        b, t, k = x.shape
        h = Wq.shape[1] // k
        scale = k ** (-0.25)
        q = (x @ Wq).reshape(b, t, h, k).transpose(0, 2, 1, 3) * scale
        kk = (x @ Wk).reshape(b, t, h, k).transpose(0, 2, 1, 3) * scale
        v = (x @ Wv).reshape(b, t, h, k).transpose(0, 2, 1, 3)
        dot = jnp.einsum('bhqk,bhsk->bhqs', q, kk)
        attn = jax.nn.softmax(dot, axis=-1)
        out = jnp.einsum('bhqs,bhsk->bhqk', attn, v)
        out = out.transpose(0, 2, 1, 3).reshape(b, t, h * k)
        return out @ Wu + bu

    def _L2_ffn_ref(x, Wr, br, ln_g, ln_b, W1, b1, W2, b2):
        import jax, jax.numpy as jnp
        import numpy as np
        TOP_K = 2
        LN_EPS = 1e-05
        B, S, D = x.shape
        N = B * S
        xt = x.reshape(N, D)
        logits = xt @ Wr + br
        probs = jax.nn.softmax(logits, axis=-1)
        top_p, top_idx = jax.lax.top_k(probs, TOP_K)
        weights = top_p / top_p.sum(axis=-1, keepdims=True)
        mu = xt.mean(axis=-1, keepdims=True)
        var = ((xt - mu) ** 2).mean(axis=-1, keepdims=True)
        xn = (xt - mu) * jax.lax.rsqrt(var + LN_EPS)
        xe = xn[None, :, :] * ln_g[:, None, :] + ln_b[:, None, :]
        h = jax.nn.gelu(jnp.einsum('end,edh->enh', xe, W1) + b1[:, None, :], approximate=False)
        y = jnp.einsum('enh,ehd->end', h, W2) + b2[:, None, :]
        y_tok = jnp.transpose(y, (1, 0, 2))
        sel = jnp.take_along_axis(y_tok, top_idx[:, :, None], axis=1)
        out = (weights[:, :, None] * sel).sum(axis=1)
        return out.reshape(B, S, D)

    def _L3_attn_ref(x, norm_w, in_proj_w, conv_w, conv_b, x_proj_w, dt_proj_w, dt_proj_b, A_log, D, out_proj_w, norm_f_w):
        import jax, jax.numpy as jnp
        import numpy as np
        D_STATE = 16
        D_CONV = 4
        DT_RANK = 16
        EPS = 1e-05

        def rmsnorm(x, w):
            return x * jax.lax.rsqrt(jnp.mean(x * x, axis=-1, keepdims=True) + EPS) * w

        def selective_scan(u, dt, A, Bm, Cm, Dp):

            def step(h, inp):
                u_t, dt_t, B_t, C_t = inp
                h = jnp.exp(dt_t[..., None] * A) * h + (dt_t * u_t)[..., None] * B_t[:, None, :]
                y_t = jnp.einsum('bds,bs->bd', h, C_t)
                return (h, y_t)
            Bsz, L, dI = u.shape
            h0 = jnp.zeros((Bsz, dI, D_STATE), u.dtype)
            xs = (u.transpose(1, 0, 2), dt.transpose(1, 0, 2), Bm.transpose(1, 0, 2), Cm.transpose(1, 0, 2))
            _, ys = jax.lax.scan(step, h0, xs)
            return ys.transpose(1, 0, 2) + u * Dp

        def mamba_mixer(x, in_w, cw, cb, xp_w, dt_w, dt_b, A_log, Dp, out_w):
            xz = x @ in_w
            u, z = jnp.split(xz, 2, axis=-1)
            dI = u.shape[-1]
            uc = jax.lax.conv_general_dilated(u.transpose(0, 2, 1), cw[:, None, :], window_strides=(1,), padding=[(D_CONV - 1, 0)], dimension_numbers=('NCH', 'OIH', 'NCH'), feature_group_count=dI)
            uc = jax.nn.silu(uc.transpose(0, 2, 1) + cb)
            x_dbl = uc @ xp_w
            dt_r = x_dbl[..., :DT_RANK]
            Bm = x_dbl[..., DT_RANK:DT_RANK + D_STATE]
            Cm = x_dbl[..., DT_RANK + D_STATE:]
            dt = jax.nn.softplus(dt_r @ dt_w + dt_b)
            A = -jnp.exp(A_log)
            y = selective_scan(uc, dt, A, Bm, Cm, Dp)
            y = y * jax.nn.silu(z)
            return y @ out_w
        hidden = x
        residual = None
        n_layer = norm_w.shape[0]
        for i in range(n_layer):
            residual = hidden if residual is None else hidden + residual
            hidden = rmsnorm(residual, norm_w[i])
            hidden = mamba_mixer(hidden, in_proj_w[i], conv_w[i], conv_b[i], x_proj_w[i], dt_proj_w[i], dt_proj_b[i], A_log[i], D[i], out_proj_w[i])
        residual = hidden + residual
        return rmsnorm(residual, norm_f_w)

    def _L3_ffn_ref(x, Wr, br, W1, b1, W2, b2, gamma, beta):
        import math
        import jax, jax.numpy as jnp
        import numpy as np
        CAPACITY_FACTOR = 1.25
        TOP_K = 2
        LN_EPS = 1e-05

        def _layer_norm(x, gamma, beta):
            mu = jnp.mean(x, axis=-1, keepdims=True)
            var = jnp.var(x, axis=-1, keepdims=True)
            return (x - mu) * jax.lax.rsqrt(var + LN_EPS) * gamma + beta
        B, S, D = x.shape
        E = Wr.shape[1]
        N = B * S
        K = TOP_K
        logits = jnp.mean(x, axis=1) @ Wr + br
        routing_weights = jax.nn.softmax(logits, axis=-1)
        capacity = float(math.ceil(N * CAPACITY_FACTOR / E))
        expected_loads = routing_weights.sum(axis=0) * (N / B)
        scale = jnp.where(expected_loads > capacity, capacity / expected_loads, 1.0)
        routing_weights = jax.nn.softmax(routing_weights * scale, axis=-1)
        rw_tok = jnp.broadcast_to(routing_weights[:, None, :], (B, S, E)).reshape(N, E)
        top_w, top_i = jax.lax.top_k(rw_tok, K)
        top_w = jax.nn.softmax(top_w, axis=-1)
        xf = x.reshape(N, D)
        h = jax.nn.gelu(jnp.einsum('nd,edf->enf', xf, W1) + b1[:, None, :], approximate=False)
        y = jnp.einsum('enf,efd->end', h, W2) + b2[:, None, :]
        w_dense = jnp.zeros((N, E), x.dtype).at[jnp.arange(N)[:, None], top_i].add(top_w)
        out = jnp.einsum('ne,end->nd', w_dense, y).reshape(B, S, D)
        out = _layer_norm(out + x, gamma, beta)
        return out

    def _gn(v, G=32, eps=1e-05):
        B_, H_, W_, C_ = v.shape
        g = v.reshape(B_, H_, W_, G, C_ // G)
        m = jnp.mean(g, axis=(1, 2, 4), keepdims=True)
        s = jnp.var(g, axis=(1, 2, 4), keepdims=True)
        return ((g - m) / jnp.sqrt(s + eps)).reshape(v.shape)

    def _ln_c(v, eps=1e-06):
        m = jnp.mean(v, axis=-1, keepdims=True)
        s = jnp.var(v, axis=-1, keepdims=True)
        return (v - m) / jnp.sqrt(s + eps)

    def _ln_t(v, eps=1e-05):
        m = jnp.mean(v, axis=-1, keepdims=True)
        s = jnp.var(v, axis=-1, keepdims=True)
        return (v - m) / jnp.sqrt(s + eps)

    def _to_tokens(v):
        B_, H_, W_, C_ = v.shape
        return v.reshape(B_, H_ * W_, C_)

    def _from_tokens(t, like):
        return t.reshape(like.shape)
    x = _L0_conv_ref(x, L0_conv_W_lk, L0_conv_W_rk, L0_conv_W_lv, L0_conv_W_rv, L0_conv_W_out, L0_conv_ln_agg_g, L0_conv_ln_agg_b, L0_conv_W1, L0_conv_b1, L0_conv_W2, L0_conv_b2, L0_conv_ln2_g, L0_conv_ln2_b)
    x = x + _L1_conv_ref(_gn(x), L1_conv_Wq, L1_conv_q_bias, L1_conv_Wk, L1_conv_Wv, L1_conv_v_bias, L1_conv_Wo, L1_conv_bo)
    t = _to_tokens(x)
    t = t + _L2_attn_ref(_ln_t(t), L2_attn_Wq, L2_attn_Wk, L2_attn_Wv, L2_attn_Wu, L2_attn_bu)
    t = t + _L2_ffn_ref(_ln_t(t), L2_ffn_Wr, L2_ffn_br, L2_ffn_ln_g, L2_ffn_ln_b, L2_ffn_W1, L2_ffn_b1, L2_ffn_W2, L2_ffn_b2)
    t = t + _L3_attn_ref(_ln_t(t), L3_attn_norm_w, L3_attn_in_proj_w, L3_attn_conv_w, L3_attn_conv_b, L3_attn_x_proj_w, L3_attn_dt_proj_w, L3_attn_dt_proj_b, L3_attn_A_log, L3_attn_D, L3_attn_out_proj_w, L3_attn_norm_f_w)
    t = t + _L3_ffn_ref(_ln_t(t), L3_ffn_Wr, L3_ffn_br, L3_ffn_W1, L3_ffn_b1, L3_ffn_W2, L3_ffn_b2, L3_ffn_gamma, L3_ffn_beta)
    x = _from_tokens(t, x)
    return x

_drawn_inputs = setup_inputs


def setup_inputs(seed=0):
    import zlib

    import numpy as np

    out = dict(_drawn_inputs(seed))
    spreads = {'L0_conv_ln_agg_g': (1.0, 0.2),
     'L0_conv_ln_agg_b': (0.0, 0.1),
     'L0_conv_b1': (0.0, 0.1),
     'L0_conv_b2': (0.0, 0.1),
     'L0_conv_ln2_g': (1.0, 0.2),
     'L0_conv_ln2_b': (0.0, 0.1),
     'L2_attn_bu': (0.0, 0.1),
     'L2_ffn_br': (0.0, 0.1),
     'L2_ffn_ln_g': (1.0, 0.2),
     'L2_ffn_ln_b': (0.0, 0.1),
     'L2_ffn_b1': (0.0, 0.1),
     'L2_ffn_b2': (0.0, 0.1),
     'L3_attn_norm_w': (1.0, 0.6),
     'L3_attn_conv_b': (0.0, 0.8),
     'L3_attn_D': (1.0, 0.6),
     'L3_attn_norm_f_w': (1.0, 0.2),
     'L3_ffn_br': (0.0, 0.8),
     'L3_ffn_b1': (0.0, 0.537),
     'L3_ffn_b2': (0.0, 0.36),
     'L3_ffn_gamma': (1.0, 0.2),
     'L3_ffn_beta': (0.0, 0.1)}
    factors = {'L3_attn_in_proj_w': 8.0,
     'L3_attn_conv_w': 8.0,
     'L3_attn_x_proj_w': 8.0,
     'L3_attn_dt_proj_w': 8.0,
     'L3_attn_dt_proj_b': 8.0,
     'L3_attn_A_log': 8.0,
     'L3_attn_out_proj_w': 8.0}
    for name, (base, spread) in spreads.items():
        noise = np.random.default_rng([zlib.crc32(name.encode()), seed]).standard_normal(out[name].shape)
        drawn = base * np.exp(spread * noise) if base else spread * noise
        out[name] = jnp.asarray(drawn.astype(out[name].dtype))
    for name, factor in factors.items():
        out[name] = (out[name] * factor).astype(out[name].dtype)
    return out
```

```python
from contextlib import ExitStack

import numpy as np

import concourse.bass as bass
from concourse import mybir

F32 = mybir.dt.float32
BF16 = mybir.dt.bfloat16
ALU = mybir.AluOpType
ACT = mybir.ActivationFunctionType
AX = mybir.AxisListType

P = 128
B, GRID, D = 2, 16, 64
N = GRID * GRID
HALF = N // P
NG = HALF * B
H8 = 8
NE = 8
HID2 = 256
NL, DI, DS, RANK = 6, 128, 16, 16
SG = 4
NSG = DS // SG
UNITS = NL * B
EPS = 1e-5
CAPACITY = 80.0

LOG1P = np.polynomial.Polynomial(
    np.polynomial.chebyshev.Chebyshev.interpolate(
        lambda u: np.log1p(u) / np.maximum(u, 1e-300), 8, domain=[0, 1]).convert(
        kind=np.polynomial.Polynomial).coef)


def quadratics():
    roots = LOG1P.roots()
    upper = sorted((r for r in roots if r.imag > 0), key=lambda r: r.real)
    k2 = float(LOG1P.coef[-1]) ** (1.0 / len(upper))
    k = k2 ** 0.5
    return [(k, -k * r.real, k2 * r.imag ** 2) for r in upper]


class Columns:

    def __init__(self, blocks):
        self.at, self.size = {}, 0
        for name, n in blocks:
            self.at[name] = (self.size, n)
            self.size += n

    def of(self, tensor, name, rows=P):
        a, n = self.at[name]
        return tensor[0:rows, a:a + n]


CONST = Columns([("ident", P), ("heads", P), ("pairs", P), ("rope", 4 * N),
                 ("fold", D), ("experts", 4 * P), ("before", NE * NE), ("pick", 32)])
W0 = Columns([("lk", P), ("lv", P), ("rk", P), ("rv", P), ("out", P), ("w1", P), ("w2", D), ("b1", 1)])
W1 = Columns([("q", P), ("qs", P), ("k", P), ("ks", P), ("v", P), ("o", 2 * D), ("qb", 1), ("qsb", 1)])
W2 = Columns([("q", 512), ("k", 512), ("v", 512), ("u", 4 * D)])
W3 = Columns([("wr", NE), ("w1", NE * HID2), ("w2", 2 * NE * D), ("b1", 2 * NE), ("g", NE), ("b", NE), ("b2", D)])
W5 = Columns([("wr", B * NE), ("w1", NE * P), ("w2", NE * D), ("b1", NE), ("b2", D)])
WM = Columns([("inu", P), ("cw", 2 * P), ("inz", P), ("xp", 112), ("dtw", P), ("out", D),
              ("alog", DS), ("cb", 1), ("dtb", 1), ("d", 1), ("norm", 1)])
ROWS = Columns([(n, D) for n in ("agg_g", "agg_b", "b2", "ln2_g", "ln2_b", "vb", "bo", "bu", "normf",
                                 "gamma", "beta")] + [("br2", NE), ("br3", NE)])


def hybrid(nc, x, const, w0, w1, w2, w3, w5, wm, rows, out):
    ctx = ExitStack()
    with ctx:
        def sb(name, shape, dt=F32):
            return ctx.enter_context(nc.sbuf_tensor(name, shape, dt))

        sems = {}

        def sem(name):
            if name not in sems:
                sems[name] = ctx.enter_context(nc.semaphore(name))
            return sems[name]

        cst = sb("cst", [P, CONST.size])
        w0t, w1t, w2t = sb("w0t", [P, W0.size]), sb("w1t", [P, W1.size]), sb("w2t", [P, W2.size])
        w3t, w5t = sb("w3t", [P, W3.size]), sb("w5t", [P, W5.size])
        wmt = [sb(f"wmt{k}", [P, WM.size]) for k in range(2)]
        rowt = sb("rowt", [P, ROWS.size])
        X = sb("X", [P, HALF, B, D])
        Y = sb("Y", [P, HALF, B, D])
        Z = sb("Z", [P, HALF, B, D])
        T2a = sb("T2a", [P, N])
        T2b = sb("T2b", [P, N])
        T2d = sb("T2d", [P, B, N])
        big = sb("big", [P, 6 * 4096])
        stats = sb("stats", [P, 9, NG, 6])
        mv = sb("mv", [P, 9, NG, 2])
        lnv = sb("lnv", [P, 9, NG])
        rstd = sb("rstd", [P, 9, NG])
        small = sb("small", [P, 512])
        b1e_t = sb("b1e", [P, 2 * NE])
        b1e = b1e_t[:]
        pick_b = sb("pick_b", [P, 32], BF16)
        PS = ctx.enter_context(nc.psum_tensor("PS", [P, 8, 512], F32))

        ident = CONST.of(cst, "ident")
        rope = CONST.of(cst, "rope").rearrange("p (t n) -> p t n", t=4)
        head_mask = lambda i: CONST.of(cst, "heads")[:, 8 * i:8 * i + 1]

        def row(name):
            n = ROWS.at[name][1]
            return ROWS.of(rowt, name).unsqueeze(1).to_broadcast([P, NG, n])

        def groups(tm):
            return tm[:].rearrange("p a b c -> p (a b) c")

        Xg, Yg, Zg = groups(X), groups(Y), groups(Z)

        def half_tm(tm, a):
            return tm[:, a].rearrange("p b c -> p (b c)")

        proj = big[:, 0:1024].rearrange("p (t n) -> p t n", t=4)
        chunk = lambda n: big[:, 4096 * n:4096 * (n + 1)]
        lkrk, lvrv, shifted, expd = chunk(1), chunk(2), chunk(3), chunk(4)
        strip = lambda t, c: t[:, 512 * c:512 * (c + 1)].rearrange("p (a q) -> p a q", a=GRID)
        half_of = lambda t, h: t[:, 2048 * h:2048 * (h + 1)]
        edge_max = small[:, 0:256]
        edge_num = small[:, 256:512]
        edge_den = big[:, 1024:1280]
        mlp_hid = big[:, 1280:1792].rearrange("p (b n) -> p b n", b=B)
        probs = big[:, 0:1024].rearrange("p (s a m) -> p s a m", s=2, a=2)
        probsT = big[:, 1024:2048].rearrange("p (s a n) -> p s a n", s=2, a=2)
        rowmax = big[:, 2048:2080].rearrange("p (i a) -> p i a", a=2)
        rowsum = big[:, 2080:2112].rearrange("p (i a) -> p i a", a=2)
        rowinv = big[:, 2112:2144].rearrange("p (i a) -> p i a", a=2)
        roped = big[:, 2304:2816].rearrange("p (t n) -> p t n", t=2)
        ropet = big[:, 2816:3840].rearrange("p (t u n) -> p t u n", t=2, u=2)
        qm = big[:, 16384:20480].rearrange("p (i n) -> p i n", i=B * H8)
        vpad = big[:, 6144:7168].rearrange("p (a b h e) -> p a b h e", a=2, b=B, h=H8)
        opad = big[:, 7168:8192].rearrange("p (g n) -> p g n", g=4)
        qz = big[:, 20480:24576].rearrange("p (c j b n) -> p c j b n", c=4, j=2, b=B)
        kT = big[:, 10240:12288].rearrange("p (c b n) -> p c b n", c=4, b=B)
        v2 = big[:, 12288:14336].rearrange("p (a b e) -> p a b e", a=2, b=B)
        oT = big[:, 14336:16384].rearrange("p (c b n) -> p c b n", c=4, b=B)
        hid = big[:, 0:8192].rearrange("p (e b n) -> p e b n", e=16, b=B)
        w1g = big[:, 8192:10240]
        yT = big[:, 10496:12544].rearrange("p (e n) -> p e n", e=4)
        wT = big[0:NE, 12544:13056]
        rt = lambda n, size: big[:, 13312 + n:13312 + n + size]
        hid5 = big[:, 0:4096].rearrange("p (e b n) -> p e b n", e=NE, b=B)
        w2w = big[:, 4096:5120].rearrange("p (b e c) -> p b e c", b=B, e=NE)

        y_bank = (2, 3, 6, 7, 0, 1, 2, 3)
        y_ones, y_b2w = big[0:NE, 5120:5248], small[0:NE, 384:512]
        two = lambda name, shape, dt=F32: [sb(f"{name}{n}", shape, dt) for n in range(2)]
        halves = lambda at, n, inner: [big[:, at + n * t:at + n * (t + 1)].rearrange("p (s n) -> p s n", n=inner)
                                       for t in range(2)]
        da = halves(0, DS * N, N)
        dbu = halves(8192, SG * N, N)
        hst = halves(10240, SG * N, N)
        hc = big[:, 16384:20480].rearrange("p (g s n) -> p g s n", g=NSG, s=SG)
        sp_q = halves(14336, 4 * N, N)
        sg, zs = two("sg", [P, 2, N]), two("zs", [P, N])
        uc, gz, dt, dtu, yg = (two(n, [P, N]) for n in ("uc", "gz", "dt", "dtu", "yg"))
        sp_u, sp_m = two("sp_u", [P, N]), two("sp_m", [P, N])
        ht = two("ht", [P, N + 4])
        hs2 = two("hs2", [P, HALF, P])
        xds, stack = two("xds", [P, N]), two("stack", [P, N], BF16)
        rest = sb("rest", [96, N])
        wcv, alog, amat = two("wcv", [P, 2 * P]), two("alog", [P, DS]), two("amat", [P, DS])
        dmat = two("dmat", [P, P])
        ssq, msq, rms = two("ssq", [P, 2]), two("msq", [P, 2]), two("rms", [P, 2])
        hbias = two("hbias", [P, 1])
        half_t, power_t = sb("half_t", [P, 1]), sb("power_t", [P, 1])
        sqs = sb("sqs", [P, HALF, D])
        eps_t, zero_t, quad_t = sb("eps_t", [P, 1]), sb("zero_t", [P, 1]), sb("quad_t", [P, 4])
        yps = [PS[:, 4 + b, 0:N] for b in range(B)]
        zps = [PS[:, 4 + b, N:2 * N] for b in range(B)]
        ups = PS[:, 6, 0:N]
        Bv, Cv = (PS[:, t:t + 2].rearrange("p c (s n) -> p (c s) n", n=N) for t in (0, 2))
        xd, dtp = PS[0:112, 7, 0:N], PS[:, 7, N:2 * N]
        hidp, tr = PS[:, 7, 0:P].rearrange("p (a c) -> p a c", a=HALF), PS[:, 7, P:P + N]

        def layer_loaded(eng, i, s):
            eng.wait_ge(sem(f"ld_wm{(s // 2) % 2}"), i * 16 + 16 * (s // 4 + 1))

        block = ctx.enter_context(nc.Block())

        @block.sync
        def _(sp):
            xin = x.rearrange("b (a r) c d -> (r c) a b d", a=HALF)
            for a in range(HALF):
                sp.dma_start(X[:, a], xin[:, a]).then_inc(sem("ld_x"), 16)
            nid = CONST.at["rope"][0]
            sp.dma_start(cst[:, 0:nid], const[:, 0:nid]).then_inc(sem("ld_ident"), 16)
            sp.dma_start(w0t[:], w0).then_inc(sem("ld_w0"), 16)
            sp.dma_start(rowt[:], rows.partition_broadcast(P)).then_inc(sem("ld_rows"), 16)
            sp.dma_start(cst[:, nid:], const[:, nid:]).then_inc(sem("ld_const"), 16)
            sp.dma_start(w1t[:], w1).then_inc(sem("ld_w1"), 16)
            sp.dma_start(w2t[:], w2).then_inc(sem("ld_w2"), 16)
            sp.dma_start(w3t[:], w3).then_inc(sem("ld_w3"), 16)
            for k in range(2):
                sp.dma_start(wmt[k][:], wm[k]).then_inc(sem(f"ld_wm{k}"), 16)
            sp.dma_start(w5t[:], w5).then_inc(sem("ld_w5"), 16)
            with sp.Fori(0, (NL - 2) // 2) as i:
                for k in range(2):
                    sp.wait_ge(sem("m_hid"), i * 4 + 2 * k + 2)
                    sp.dma_start(wmt[k][:], wm[i * 2 + k + 2]).then_inc(sem(f"ld_wm{k}"), 16)
            sp.wait_ge(sem("result"), 1)
            oview = out.rearrange("b (a r) c d -> (r c) a b d", a=HALF)
            for a in range(HALF):
                sp.dma_start(oview[:, a], Z[:, a]).then_inc(sem("stored"), 16)
            sp.wait_ge(sem("stored"), 16 * HALF)

        @block.tensor
        def _(pe):
            def to_T2(src, dst, ready, count, done):
                pe.wait_ge(sem(ready), count)
                for a in range(HALF):
                    last = pe.transpose(dst[:, a * P:(a + 1) * P], half_tm(src, a), ident)
                last.then_inc(sem(done), 1)

            pe.wait_ge(sem("ld_x"), 16 * HALF)
            to_T2(X, PS[:, 0, 0:N], "ld_ident", 16, "e_xT")
            pe.wait_ge(sem("ld_w0"), 16)
            pe.wait_ge(sem("e_xTs"), 1)
            for t, name in enumerate(("lk", "rk", "lv", "rv")):
                last = pe.matmul(PS[:, 1 + t // 2, (t % 2) * N:(t % 2 + 1) * N], W0.of(w0t, name), T2a[:],
                                 start=True, stop=True)
                if t % 2:
                    last.then_inc(sem("e_proj"), 1)
            for c in range(8):
                pe.wait_ge(sem("e_lkrk"), c + 1)
                if c == 0:
                    pe.wait_ge(sem("e_projs"), 2)
                pe.matmul(PS[:, c], CONST.of(cst, "heads"), lkrk[:, 512 * c:512 * (c + 1)], start=True, stop=True)\
                    .then_inc(sem("e_score"), 1)
            for h in range(2):
                pe.wait_ge(sem("e_exp"), 4 * h + 4)
                exps = half_of(expd, h).rearrange("p (c a q) -> p a c q", c=4, a=GRID)
                for a in range(GRID):
                    last = pe.matmul(PS[:, h, 0:P].rearrange("p (c q) -> p c q", c=4), ident, exps[:, a],
                                     start=(a == 0), stop=(a == GRID - 1))
                last.then_inc(sem("e_den"), 1)
            pe.wait_ge(sem("ld_w3"), 16)
            w1raw = W3.of(w3t, "w1")
            for e in range(2 * NE):
                last = pe.matmul(PS[:, 2, e:e + 1], w1raw[0:64, e * P:(e + 1) * P],
                                 W3.of(w3t, "b")[0:64, e // 2:e // 2 + 1], start=True, stop=True)
            last.then_inc(sem("x_b1"), 1)
            pe.wait_ge(sem("e_o"), 1)
            for a in range(HALF):
                last = pe.matmul(PS[:, 1, a * P:(a + 1) * P], edge_num[:, a * P:(a + 1) * P], W0.of(w0t, "out"),
                                 start=True, stop=True)
            last.then_inc(sem("e_out"), 1)
            to_T2(Y, PS[:, 2, 0:N], "ln_out", 2, "f0_T")
            pe.wait_ge(sem("f0_Ts"), B)
            pe.matmul(PS[:, 3], W0.of(w0t, "w1"), T2d[:].rearrange("p b n -> p (b n)"), start=True, stop=True)\
                .then_inc(sem("f0_h"), 1)
            pe.wait_ge(sem("f0_relu"), 1)
            for a in range(HALF):
                for b in range(B):
                    g = a * B + b
                    last = pe.matmul(PS[:, 4, g * D:(g + 1) * D], mlp_hid[:, b, a * P:(a + 1) * P],
                                     W0.of(w0t, "w2"), start=True, stop=True)
            last.then_inc(sem("f0_y"), 1)

            to_T2(X, PS[:, 5, 0:N], "ln_out", 4, "g_T")
            pe.wait_ge(sem("g_stats"), 1)
            pe.matmul(PS[:, 6, 0:2], CONST.of(cst, "pairs"), small[:, 0:2], start=True, stop=True).then_inc(
                sem("g_pair"), 1)
            pe.wait_ge(sem("g_x"), 1)
            pe.wait_ge(sem("ld_w1"), 16)
            for t, name in enumerate(("q", "qs", "k", "ks")):
                last = pe.matmul(PS[:, t // 2, (t % 2) * N:(t % 2 + 1) * N], W1.of(w1t, name), T2a[:],
                                 start=True, stop=True)
                if t % 2:
                    last.then_inc(sem("r_proj"), 1)
            for a in range(HALF):
                last = pe.matmul(PS[:, 2, a * P:(a + 1) * P], T2a[:, a * P:(a + 1) * P], W1.of(w1t, "v"),
                                 start=True, stop=True)
            last.then_inc(sem("r_v"), 1)
            def attention(base, score_ops, value_ops):
                n = B * H8
                for i in range(-2, n + 1):
                    if i + 2 < n:
                        if i >= 0:
                            pe.wait_ge(sem("h_exp"), 2 * base + 2 * i + 2)
                        score_ops(i + 2).then_inc(sem("h_score"), 1)
                    if 0 <= i < n:
                        pe.wait_ge(sem("h_norm"), 2 * base + 2 * i + 2)
                        if i >= 2:
                            pe.wait_ge(sem("h_pT"), base + i - 1)
                        for a in range(2):
                            for m in range(2):
                                last = pe.transpose(PS[:, 2 + i % 2, m * N + a * P:m * N + (a + 1) * P],
                                                    probs[:, i % 2, a, m * P:(m + 1) * P], ident)
                        last.then_inc(sem("h_t"), 1)
                    if i >= 1:
                        pe.wait_ge(sem("h_pT"), base + i)
                        value_ops(i - 1).then_inc(sem("h_av"), 1)

            def r_scores(i):
                if i == 0:
                    pe.wait_ge(sem("r_rope"), 2)
                pe.wait_ge(sem("r_qm"), i + 1)
                for a in range(2):
                    last = pe.matmul(PS[:, i % 2, a * N:(a + 1) * N], qm[:, i, a * P:(a + 1) * P], roped[:, 1],
                                     start=True, stop=True)
                return last

            def r_values(i):
                b, h = divmod(i, H8)
                g, j = 2 * b + h // 4, 32 * (h % 4)
                if i == 0:
                    pe.wait_ge(sem("r_vs"), 3)
                for m in range(2):
                    last = pe.matmul(PS[j:j + 32, 4 + g // 2, (g % 2) * N:(g % 2 + 1) * N], vpad[:, m, b, h],
                                     probsT[:, i % 2, m], start=(m == 0), stop=(m == 1))
                return last

            attention(0, r_scores, r_values)
            pe.wait_ge(sem("r_oT"), 2)
            wo = W1.of(w1t, "o").rearrange("p (g c) -> p g c", g=2)
            for a in range(HALF):
                for b in range(B):
                    gr = a * B + b
                    for g in range(2):
                        last = pe.matmul(PS[:, 6, gr * D:(gr + 1) * D], opad[:, 2 * b + g, a * P:(a + 1) * P],
                                         wo[:, g], start=(g == 0), stop=(g == 1))
            last.then_inc(sem("r_out"), 1)

            to_T2(Y, PS[:, 7, 0:N], "ln_norm", 3 * NG, "a_T")
            pe.wait_ge(sem("a_Ts"), B)
            pe.wait_ge(sem("ld_w2"), 16)
            both = T2d[:].rearrange("p b n -> p (b n)")
            for t, name in enumerate(("q", "k")):
                for c in range(4):
                    if t == 1:
                        pe.wait_ge(sem("a_q"), 2 * c + 2)
                    pe.matmul(PS[:, c], W2.of(w2t, name)[:, c * P:(c + 1) * P], both, start=True, stop=True)\
                        .then_inc(sem("a_proj"), 1)
            for a in range(HALF):
                for b in range(B):
                    pe.matmul(PS[:, 4 + a * B + b], T2d[:, b, a * P:(a + 1) * P], W2.of(w2t, "v"),
                              start=True, stop=True).then_inc(sem("a_v"), 1)

            def a_scores(i):
                b, h = divmod(i, H8)
                c = h // 2
                if i == 0:
                    pe.wait_ge(sem("a_k"), 4)
                for a in range(2):
                    last = pe.matmul(PS[:, i % 2, a * N:(a + 1) * N], qz[:, c, h % 2, b, a * P:(a + 1) * P],
                                     kT[:, c, b], start=True, stop=True)
                return last

            def a_values(i):
                b, h = divmod(i, H8)
                c, j = h // 2, 64 * (h % 2)
                if i == 0:
                    pe.wait_ge(sem("a_vs"), NG)
                for m in range(2):
                    last = pe.matmul(PS[j:j + 64, 4 + c, b * N:(b + 1) * N], v2[:, m, b, h * D:(h + 1) * D],
                                     probsT[:, i % 2, m], start=(m == 0), stop=(m == 1))
                return last

            attention(B * H8, a_scores, a_values)
            pe.wait_ge(sem("a_oT"), 4)
            wu = W2.of(w2t, "u").rearrange("p (c e) -> p c e", c=4)
            for a in range(HALF):
                for b in range(B):
                    gr = a * B + b
                    for c in range(4):
                        last = pe.matmul(PS[:, 0, gr * D:(gr + 1) * D], oT[:, c, b, a * P:(a + 1) * P],
                                         wu[:, c], start=(c == 0), stop=(c == 3))
            last.then_inc(sem("a_out"), 1)

            to_T2(Y, PS[:, 2, 0:N], "ln_norm", 4 * NG, "x_T")
            to_T2(Z, PS[:, 3, 0:N], "ln_norm", 5 * NG, "x_nT")
            pe.wait_ge(sem("x_Ts"), 1)
            for a in range(HALF):
                for b in range(B):
                    g = a * B + b
                    last = pe.matmul(PS[:, b, 32 + a * NE:32 + (a + 1) * NE], T2a[64 * b:64 * b + 64, a * P:(a + 1) * P],
                                     W3.of(w3t, "wr")[64 * b:64 * b + 64], start=True, stop=True)
            last.then_inc(sem("x_logit"), 1)
            pe.wait_ge(sem("x_nTs"), B)
            pe.wait_ge(sem("x_w1g"), NE)
            for e in range(2 * NE):
                if e >= 4:
                    pe.wait_ge(sem("x_gelu"), e - 3)
                pe.matmul(PS[:, 4 + e % 4], w1g[:, e * P:(e + 1) * P], both, start=True, stop=True)\
                    .then_inc(sem("x_h"), 1)
            pe.wait_ge(sem("x_w"), 1)
            pe.wait_ge(sem("x_gelu"), 13)
            for g in range(NG):
                a, b = divmod(g, B)
                last = pe.transpose(PS[0:NE, 4, b * N + a * P:b * N + (a + 1) * P], rt(64 + g * NE, NE), ident)
            last.then_inc(sem("x_wT"), 1)
            w2x = W3.of(w3t, "w2").rearrange("p (e c) -> p e c", e=2 * NE)
            selE = CONST.of(cst, "experts", NE).rearrange("p (t n) -> p t n", t=4)
            for pair in range(4):
                for r in range(2):
                    for ch in range(2):
                        e = (2 * pair + r) * 2 + ch
                        pe.wait_ge(sem("x_gelu"), e + 1)
                        last = pe.matmul(PS[64 * r:64 * r + 64, pair], w2x[:, e],
                                         hid[:, e].rearrange("p b n -> p (b n)"), start=(ch == 0), stop=(ch == 1))
                last.then_inc(sem("x_y"), 1)
                if pair == 0:
                    pe.wait_ge(sem("x_wTs"), 1)
                    pe.wait_ge(sem("x_gelu"), 2 * NE)
                if pair >= 2:
                    pe.wait_ge(sem("x_wide"), pair - 1)
                pe.matmul(PS[:, 5 + pair % 2], selE[:, pair], wT, start=True, stop=True).then_inc(sem("x_wbc"), 1)
            for g in range(NG):
                a, b = divmod(g, B)
                cols = slice(b * N + a * P, b * N + (a + 1) * P)
                pe.matmul(PS[:, 7, g * D:(g + 1) * D], wT[:, cols], W3.of(w3t, "b2", NE), start=True, stop=False)
                if g == 0:
                    pe.wait_ge(sem("x_yw"), 7)
                last = pe.matmul(PS[:, 7, g * D:(g + 1) * D], yT[:, 0, cols], CONST.of(cst, "fold"),
                                 start=False, stop=True)
            last.then_inc(sem("x_out"), 1)

            def prep_transpose(u, k, b):
                pe.wait_ge(sem("m_hs"), u + 1)
                for a in range(HALF):
                    last = pe.transpose(tr[:, a * P:(a + 1) * P], hs2[b][:, a], ident)
                last.then_inc(sem("m_tr"), 1)

            def prep_in(u, k, b, layers):
                pe.wait_ge(sem("m_ht"), u * 2 + 2)
                pe.wait_ge(sem("m_wc"), layers)
                pe.matmul(ups, wcv[k][:, 0:P], ht[b][:, 3:3 + N], start=True, stop=False)
                pe.matmul(ups, wcv[k][:, P:2 * P], ht[b][:, 1:1 + N], start=False, stop=True).then_inc(sem("m_up"), 1)
                pe.matmul(zps[b], WM.of(wmt[k], "inz", 64), ht[b][0:64, 3:3 + N], start=True, stop=True)\
                    .then_inc(sem("m_zp"), 1)

            def prep_x(u, k, b):
                pe.wait_ge(sem("m_uc"), u + 1)
                pe.matmul(xd, WM.of(wmt[k], "xp"), uc[b][:], start=True, stop=True).then_inc(sem("m_xd"), 1)

            def prep_dt(u, k, b):
                pe.wait_ge(sem("m_xds"), u + 1)
                pe.matmul(dtp, WM.of(wmt[k], "dtw")[96:112], xds[b][96:112], start=True, stop=True).then_inc(sem("m_dtp"), 1)

            def spread(bank, column, b, done):
                for n in range(SG):
                    last = pe.matmul(PS[:, bank + n // 2, (n % 2) * N:(n % 2 + 1) * N],
                                     pick_b[0:96, column + n:column + n + 1].to_broadcast([96, P]),
                                     stack[b][0:96], start=True, stop=True)
                last.then_inc(sem(done), 1)

            def spread_b(u, b, g):
                if g == 0:
                    pe.wait_ge(sem("m_stack"), u + 1)
                spread(0, SG * g, b, "m_B")

            def spread_c(b, g):
                spread(2, DS + SG * g, b, "m_C")

            def sum_first(u, k, b, half):
                if half == 0:
                    pe.wait_ge(sem("m_zs"), u + 1)
                    pe.matmul(yps[b], dmat[k][:], uc[b][:], start=True, stop=False)
                    pe.wait_ge(sem("m_pair"), u + 1)
                for s in range(2 * half, 2 * half + 2):
                    pe.matmul(yps[b], ident, hc[:, 0, s], start=False, stop=False)

            def sum_y(u, b, g):
                pe.wait_ge(sem("m_hc"), u * NSG + g + 1)
                for s in range(SG):
                    last = pe.matmul(yps[b], ident, hc[:, g, s], start=False,
                                     stop=(g == NSG - 1 and s == SG - 1))
                if g == NSG - 1:
                    last.then_inc(sem("m_y"), 1)

            def out_proj(u, k, b):
                pe.wait_ge(sem("m_gate"), u + 1)
                for a in range(HALF):
                    last = pe.matmul(hidp[:, a], yg[b][:, a * P:(a + 1) * P], WM.of(wmt[k], "out"),
                                     start=True, stop=True)
                last.then_inc(sem("m_hid"), 1)

            def pe_step(i, s, first=False, last=False):
                u = i * 4 + s
                k, b = (s // 2) % 2, s % 2
                nk, nb = ((s + 1) // 2) % 2, (s + 1) % 2
                pk = ((s - 1) // 2) % 2
                if not first:
                    sum_y(u + -1, nb, NSG - 1)
                    pe.wait_ge(sem("m_dbu"), u * NSG)
                    pe.wait_ge(sem("m_hc"), u * NSG)
                spread_b(u, b, 0)
                spread_c(b, 0)
                if not first:
                    out_proj(u + -1, pk, nb)
                pe.wait_ge(sem("m_dbu"), u * NSG + 1)
                spread_b(u, b, 1)
                if not last:
                    prep_transpose(u + 1, nk, nb)
                pe.wait_ge(sem("m_hc"), u * NSG + 1)
                spread_c(b, 1)
                pe.wait_ge(sem("m_dbu"), u * NSG + 2)
                spread_b(u, b, 2)
                if not last:
                    prep_in(u + 1, nk, nb, i * 2 + (s + 1) // 2 + 1)
                pe.wait_ge(sem("m_hc"), u * NSG + 2)
                spread_c(b, 2)
                pe.wait_ge(sem("m_dbu"), u * NSG + 3)
                spread_b(u, b, 3)
                sum_first(u, k, b, 0)
                if not last:
                    prep_x(u + 1, nk, nb)
                sum_first(u, k, b, 1)
                if not last:
                    prep_dt(u + 1, nk, nb)
                pe.wait_ge(sem("m_hc"), u * NSG + 3)
                spread_c(b, 3)
                sum_y(u, b, 2)

            prep_transpose(0, 0, 0)
            prep_in(0, 0, 0, 1)
            prep_x(0, 0, 0)
            prep_dt(0, 0, 0)
            pe_step(0, 0, first=True)
            with pe.Fori(0, 2) as i:
                for s in range(1, 5):
                    pe_step(i, s)
            for s in range(9, 12):
                pe_step(0, s, last=(s == 11))
            sum_y(UNITS - 1, 1, NSG - 1)
            out_proj(UNITS - 1, 1, 1)

            to_T2(Y, PS[:, 0, 0:N], "ln_norm", 7 * NG, "y_T")
            pe.wait_ge(sem("y_mean"), 1)
            pe.wait_ge(sem("ld_w5"), 16)
            pe.matmul(PS[:, 1, 0:B * NE], small[:, 16:17].to_broadcast([P, P]), W5.of(w5t, "wr"),
                      start=True, stop=True).then_inc(sem("y_logit"), 1)
            pe.wait_ge(sem("y_Ts"), B)
            for e in range(NE):
                if e == 5:
                    pe.wait_ge(sem("y_shift"), 1)
                if e >= 6:
                    pe.wait_ge(sem("y_gelu"), e - 5)
                pe.matmul(PS[:, y_bank[e]], W5.of(w5t, "w1")[:, e * P:(e + 1) * P], both,
                          start=True, stop=True).then_inc(sem("y_h"), 1)
            pe.wait_ge(sem("y_w2w"), 2)
            for e in range(NE):
                pe.wait_ge(sem("y_gelu"), e + 1)
                for b in range(B):
                    last = pe.matmul(PS[64 * b:64 * b + 64, 4, 0:N], w2w[:, b, e], hid5[:, e, b],
                                     start=(e == 0), stop=(e == NE - 1))
            last.then_inc(sem("y_y"), 1)
            pe.wait_ge(sem("y_ys"), 1)
            pe.wait_ge(sem("y_b2w"), 1)
            for a in range(HALF):
                last = pe.matmul(PS[:, 5, a * P:(a + 1) * P], T2b[:, a * P:(a + 1) * P], ident,
                                 start=True, stop=False)
                last = pe.matmul(PS[:, 5, a * P:(a + 1) * P], y_ones, y_b2w, start=False, stop=True)
            last.then_inc(sem("y_out"), 1)

        @block.vector
        def _(v):
            def ln(j, src, dst, gain=None, shift=None):
                for g in range(NG):
                    v.bn_stats(stats[:, j, g], src[:, g]).then_inc(sem("ln_stats"), 1)
                for g in range(NG):
                    v.wait_ge(sem("ln_stats"), j * NG + g + 1)
                    v.bn_aggr(mv[:, j, g], stats[:, j, g]).then_inc(sem("ln_aggr"), 1)
                v.wait_ge(sem("ln_rstd"), j + 1)
                for g in range(NG):
                    v.tensor_scalar(dst[:, g], src[:, g], mv[:, j, g, 0:1], rstd[:, j, g:g + 1],
                                    ALU.subtract, ALU.mult).then_inc(sem("ln_norm"), 1)
                if gain is not None:
                    v.wait_ge(sem("ld_rows"), 16)
                    v.wait_ge(sem("ln_norm"), (j + 1) * NG)
                    v.tensor_tensor(dst, dst, row(gain), ALU.mult).then_inc(sem("ln_out"), 1)
                    v.wait_ge(sem("ln_out"), {0: 1, 1: 3, 7: 5}[j])
                    v.tensor_tensor(dst, dst, row(shift), ALU.add).then_inc(sem("ln_out"), 1)

            def apart(src, done):
                for b in range(B):
                    v.tensor_copy(T2d[64 * b:64 * b + 64, b], src[64 * b:64 * b + 64]).then_inc(sem(done), 1)

            steps = [0]

            def chain(ins):
                steps[0] += 1
                ins.then_inc(sem("v_chain"), 1)
                v.wait_ge(sem("v_chain"), steps[0])

            v.wait_ge(sem("e_xT"), 1)
            v.tensor_copy(T2a[:], PS[:, 0, 0:N]).then_inc(sem("e_xTs"), 1)
            v.wait_ge(sem("e_projs"), 1)

            for c in range(8):
                l = proj[:, 0].rearrange("p (x a) -> p a x", a=GRID)[:, :, 2 * c:2 * c + 2]
                r = proj[:, 1].rearrange("p (a y) -> p a y", a=GRID)
                v.tensor_tensor(strip(lkrk, c).rearrange("p a (x y) -> p a x y", y=GRID),
                                l.unsqueeze(3).to_broadcast([P, GRID, 2, GRID]),
                                r.unsqueeze(2).to_broadcast([P, GRID, 2, GRID]), ALU.mult).then_inc(sem("e_lkrk"), 1)
            for c in range(9):
                if c < 8:
                    v.wait_ge(sem("e_score"), c + 1)
                    v.tensor_reduce(edge_max[:, 32 * c:32 * c + 32],
                                    PS[:, c].rearrange("p (a q) -> p q a", a=GRID), AX.X, ALU.max)\
                        .then_inc(sem("e_max"), 1)
                if c > 0:
                    d = c - 1
                    v.wait_ge(sem("e_max"), c)
                    m = edge_max[:, 32 * d:32 * d + 32].unsqueeze(1).to_broadcast([P, GRID, 32])
                    v.tensor_tensor(strip(shifted, d), PS[:, d].rearrange("p (a q) -> p a q", a=GRID), m,
                                    ALU.subtract).then_inc(sem("e_shift"), 1)
            v.wait_ge(sem("e_exp"), 4)
            v.wait_ge(sem("e_lvrv"), 4)
            chain(v.tensor_tensor(half_of(shifted, 0), half_of(expd, 0), half_of(lvrv, 0), ALU.mult))
            for h in range(2):
                if h:
                    v.wait_ge(sem("e_ev"), 1)
                v.tensor_reduce(edge_num[:, h * P:(h + 1) * P].rearrange("p (c q) -> p c q", c=4),
                                half_of(shifted, h).rearrange("p (c a q) -> p c q a", c=4, a=GRID),
                                AX.X, ALU.add).then_inc(sem("e_num"), 1)
                v.wait_ge(sem("e_den"), h + 1)
                v.reciprocal(edge_den[:, h * P:(h + 1) * P], PS[:, h, 0:P]).then_inc(sem("e_num"), 1)
            v.wait_ge(sem("e_num"), 4)
            v.tensor_tensor(edge_num, edge_num, edge_den, ALU.mult).then_inc(sem("e_o"), 1)
            v.wait_ge(sem("x_b1"), 1)
            v.tensor_tensor(b1e, W3.of(w3t, "b1"), PS[:, 2, 0:16], ALU.add).then_inc(sem("x_b1s"), 1)
            v.wait_ge(sem("e_out"), 1)
            chain(v.tensor_tensor(Yg, Xg, PS[:, 1, 0:NG * D].rearrange("p (g c) -> p g c", g=NG), ALU.add))
            ln(0, Yg, Yg, "agg_g", "agg_b")
            v.wait_ge(sem("f0_T"), 1)
            apart(PS[:, 2, 0:N], "f0_Ts")
            chain(v.tensor_tensor(Yg, Yg, row("b2"), ALU.add))
            v.wait_ge(sem("f0_y"), 1)
            chain(v.tensor_tensor(Xg, Yg, PS[:, 4, 0:NG * D].rearrange("p (g c) -> p g c", g=NG), ALU.add))
            ln(1, Xg, Xg, "ln2_g", "ln2_b")

            v.wait_ge(sem("g_T"), 1)
            xT = PS[:, 5, 0:N]
            chain(v.bn_stats(stats[:, 8, 0], xT))
            chain(v.bn_aggr(mv[:, 8, 0], stats[:, 8, 0]))
            chain(v.tensor_copy(small[:, 0:1], mv[:, 8, 0, 0:1]))
            v.scalar_tensor_tensor(small[:, 1:2], mv[:, 8, 0, 0:1], mv[:, 8, 0, 0:1], mv[:, 8, 0, 1:2],
                                   ALU.mult, ALU.add).then_inc(sem("g_stats"), 1)
            v.wait_ge(sem("g_pair"), 1)
            chain(v.tensor_copy(small[:, 2:4], PS[:, 6, 0:2]))
            chain(v.tensor_tensor(small[:, 4:5], small[:, 2:3], small[:, 2:3], ALU.mult))
            v.tensor_tensor(small[:, 5:6], small[:, 3:4], small[:, 4:5], ALU.subtract).then_inc(sem("g_var"), 1)
            v.wait_ge(sem("g_rstd"), 1)
            v.tensor_scalar(T2a[:], xT, small[:, 2:3], small[:, 7:8], ALU.subtract, ALU.mult)\
                .then_inc(sem("g_x"), 1)
            v.wait_ge(sem("ld_const"), 16)
            bias = ("qb", "qsb")
            for t in range(2):
                v.wait_ge(sem("r_proj"), t + 1)
                for s in range(2):
                    src = PS[:, t, s * N:(s + 1) * N]
                    if t == 0:
                        v.scalar_tensor_tensor(ropet[:, t, s], src, W1.of(w1t, bias[s]), rope[:, 2 * t + s],
                                               ALU.add, ALU.mult).then_inc(sem("r_half"), 1)
                    else:
                        v.tensor_tensor(ropet[:, t, s], src, rope[:, 2 * t + s], ALU.mult)\
                            .then_inc(sem("r_half"), 1)
                v.wait_ge(sem("r_half"), 2 * t + 2)
                v.tensor_tensor(roped[:, t], ropet[:, t, 0], ropet[:, t, 1], ALU.add).then_inc(sem("r_rope"), 1)
            v.wait_ge(sem("r_v"), 1)
            vb = ROWS.of(rowt, "vb").rearrange("p (h e) -> p h e", h=H8)
            v.wait_ge(sem("r_vs"), 1)
            for a in range(HALF):
                v.tensor_tensor(vpad[:, a, :, :, 0:8],
                                PS[:, 2, a * P:(a + 1) * P].rearrange("p (b h e) -> p b h e", b=B, h=H8),
                                vb.unsqueeze(1).to_broadcast([P, B, H8, 8]), ALU.add).then_inc(sem("r_vs"), 1)

            def attention(base):
                n = B * H8
                for i in range(n + 1):
                    if i < n:
                        v.wait_ge(sem("h_score"), base + i + 1)
                        v.tensor_reduce(rowmax[:, i], PS[:, i % 2].rearrange("p (a m) -> p a m", a=2), AX.X,
                                        ALU.max, negate=True).then_inc(sem("h_max"), 1)
                    if i >= 1:
                        j = i - 1
                        v.wait_ge(sem("h_exp"), 2 * base + 2 * j + 2)
                        v.reciprocal(rowinv[:, j], rowsum[:, j]).then_inc(sem("h_inv"), 1)
                        v.wait_ge(sem("h_inv"), base + j + 1)
                        for a in range(2):
                            v.tensor_scalar(probs[:, j % 2, a], probs[:, j % 2, a], rowinv[:, j, a:a + 1], None,
                                            ALU.mult).then_inc(sem("h_norm"), 1)

            attention(0)
            v.wait_ge(sem("h_av"), B * H8)
            v.tensor_copy(opad[:, 0:2].rearrange("p g n -> p (g n)"), PS[:, 4]).then_inc(sem("r_oT"), 1)
            chain(v.tensor_tensor(Xg, Xg, row("bo"), ALU.add))
            v.wait_ge(sem("r_out"), 1)
            chain(v.tensor_tensor(Xg, Xg, PS[:, 6, 0:NG * D].rearrange("p (g c) -> p g c", g=NG), ALU.add))
            ln(2, Xg, Yg)
            v.wait_ge(sem("a_T"), 1)
            apart(PS[:, 7, 0:N], "a_Ts")
            for c in range(4):
                v.wait_ge(sem("a_proj"), c + 5)
                v.tensor_copy(kT[:, c].rearrange("p b n -> p (b n)"), PS[:, c]).then_inc(sem("a_k"), 1)
            for a in range(HALF):
                for b in range(B):
                    g = a * B + b
                    v.wait_ge(sem("a_v"), g + 1)
                    v.tensor_copy(v2[:, a, b], PS[:, 4 + g]).then_inc(sem("a_vs"), 1)
            attention(B * H8)
            v.wait_ge(sem("h_av"), 2 * B * H8)
            for c in range(2):
                v.tensor_copy(oT[:, c].rearrange("p b n -> p (b n)"), PS[:, 4 + c]).then_inc(sem("a_oT"), 1)
            chain(v.tensor_tensor(Xg, Xg, row("bu"), ALU.add))
            v.wait_ge(sem("a_out"), 1)
            chain(v.tensor_tensor(Xg, Xg, PS[:, 0, 0:NG * D].rearrange("p (g c) -> p g c", g=NG), ALU.add))

            ln(3, Xg, Yg)
            v.wait_ge(sem("ln_norm"), 4 * NG)
            ln(4, Yg, Zg)
            v.wait_ge(sem("x_T"), 1)
            v.tensor_copy(T2a[:], PS[:, 2, 0:N]).then_inc(sem("x_Ts"), 1)
            v.wait_ge(sem("x_nT"), 1)
            apart(PS[:, 3, 0:N], "x_nTs")
            per = lambda ap, n=NG: ap.rearrange("p (g e) -> p g e", g=n)

            def over(ap, n=NG):
                return ap.unsqueeze(2).to_broadcast([P, n, NE])

            def softmax_shift(dst, src, top, n):
                chain(v.tensor_reduce(top, per(src, n), AX.X, ALU.max))
                chain(v.tensor_tensor(per(dst, n), per(src, n), over(top, n), ALU.subtract))

            def top2(mask, p, n, gt, eq):
                sh = [P, n, NE, NE]
                mine = per(p, n).unsqueeze(3).to_broadcast(sh)
                other = per(p, n).unsqueeze(2).to_broadcast(sh)
                view = lambda t: t.rearrange("p (g e j) -> p g e j", g=n, e=NE)
                before = CONST.of(cst, "before").rearrange("p (e j) -> p e j", e=NE).unsqueeze(1).to_broadcast(sh)
                v.tensor_tensor(view(gt), other, mine, ALU.is_gt).then_inc(sem("v_gt"), 1)
                chain(v.tensor_tensor(view(eq), other, mine, ALU.is_equal))
                chain(v.tensor_tensor(view(eq), view(eq), before, ALU.mult))
                chain(v.tensor_tensor(gt, gt, eq, ALU.add))
                chain(v.tensor_reduce(mask, view(gt), AX.X, ALU.add))
                chain(v.tensor_scalar(mask, mask, 1.5, None, ALU.is_lt))

            lg, pr, wts, msk = rt(0, 32), rt(32, 32), rt(64, 32), rt(96, 32)
            sc4, gt2, eq2 = rt(128, 4), rt(160, 256), rt(416, 256)
            v.wait_ge(sem("x_logit"), 1)
            for b in range(B):
                chain(v.tensor_tensor(lg.rearrange("p (a b e) -> p a b e", a=HALF, b=B)[:, :, b],
                                      PS[:, b, 32:48].rearrange("p (a e) -> p a e", a=HALF),
                                      ROWS.of(rowt, "br2").unsqueeze(1).to_broadcast([P, HALF, NE]), ALU.add))
            softmax_shift(lg, lg, sc4, NG)
            v.sem_inc(sem("x_shift"), 1)
            v.wait_ge(sem("x_exp"), 1)
            chain(v.tensor_reduce(sc4, per(pr), AX.X, ALU.add))
            chain(v.reciprocal(sc4, sc4))
            chain(v.tensor_tensor(per(pr), per(pr), over(sc4), ALU.mult))
            top2(msk, pr, NG, gt2, eq2)
            chain(v.tensor_tensor(wts, msk, pr, ALU.mult))
            chain(v.tensor_reduce(sc4, per(wts), AX.X, ALU.add))
            chain(v.reciprocal(sc4, sc4))
            v.tensor_tensor(per(wts), per(wts), over(sc4), ALU.mult).then_inc(sem("x_w"), 1)
            v.wait_ge(sem("x_wT"), 1)
            v.tensor_copy(wT, PS[0:NE, 4]).then_inc(sem("x_wTs"), 1)
            wide = lambda n: big[:, 14336 + 512 * (n % 2):14336 + 512 * (n % 2 + 1)]
            for pair in range(4):
                v.wait_ge(sem("x_wide"), pair + 1)
                v.wait_ge(sem("x_y"), pair + 1)
                v.tensor_tensor(yT[:, pair], wide(pair), PS[:, pair], ALU.mult).then_inc(sem("x_yw"), 1)
                if pair:
                    v.wait_ge(sem("x_yw"), 2 * pair)
                    v.tensor_tensor(yT[:, 0], yT[:, 0], yT[:, pair], ALU.add).then_inc(sem("x_yw"), 1)
            v.wait_ge(sem("x_out"), 1)
            chain(v.tensor_tensor(Xg, Xg, PS[:, 7, 0:NG * D].rearrange("p (g c) -> p g c", g=NG), ALU.add))

            ln(5, Xg, Yg)
            v.wait_ge(sem("ln_norm"), 6 * NG)

            def prep_uc(u, k, b):
                v.wait_ge(sem("m_sig"), u * 2 + 1)
                v.scalar_tensor_tensor(uc[b][:], ups, WM.of(wmt[k], "cb"), sg[b][:, 0], ALU.add, ALU.mult)\
                    .then_inc(sem("m_uc"), 1)

            def gate(u, k, b):
                v.wait_ge(sem("m_y"), u + 1)
                v.wait_ge(sem("m_gz"), u + 1)
                v.tensor_tensor(yg[b][:], yps[b], gz[b][:], ALU.mult).then_inc(sem("m_gate"), 1)

            def residual(u, b):
                v.wait_ge(sem("m_hid"), u + 1)
                v.tensor_tensor(Y[:, :, b], Y[:, :, b], hidp, ALU.add).then_inc(sem("m_res"), 1)

            def prep_dt(u, b):
                for q in range(4):
                    cq = quadratics()[q][2]
                    v.wait_ge(sem("m_q"), u * 4 + q + 1)
                    if q > 0:
                        v.wait_ge(sem("m_poly"), u * 4 + q)
                    src = sp_u[b][:] if q == 0 else dt[b][:]
                    v.scalar_tensor_tensor(dt[b][:], sp_q[b][:, q], cq, src, ALU.add, ALU.mult)\
                        .then_inc(sem("m_poly"), 1)
                v.wait_ge(sem("m_poly"), u * 4 + 4)
                v.wait_ge(sem("m_relu"), u + 1)
                v.tensor_tensor(dt[b][:], dt[b][:], sp_m[b][:], ALU.add).then_inc(sem("m_dt"), 1)
                v.wait_ge(sem("m_dt"), u + 1)
                v.wait_ge(sem("m_uc"), u + 1)
                v.tensor_tensor(dtu[b][:], dt[b][:], uc[b][:], ALU.mult).then_inc(sem("m_dtu"), 1)

            def v_step(i, s, first=False, last=False):
                u = i * 4 + s
                k, b = (s // 2) % 2, s % 2
                nk, nb = ((s + 1) // 2) % 2, (s + 1) % 2
                pk = ((s - 1) // 2) % 2
                prep_dt(u, b)
                if not first:
                    gate(u + -1, pk, nb)
                for g in range(NSG):
                    v.wait_ge(sem("m_B"), u * NSG + g + 1)
                    if g == 0:
                        v.wait_ge(sem("m_dtu"), u + 1)
                    v.tensor_tensor(dbu[g % 2][:], dtu[b][:].unsqueeze(1).to_broadcast([P, SG, N]), Bv, ALU.mult)\
                        .then_inc(sem("m_dbu"), 1)
                    if g == 0 and not first:
                        residual(u + -1, nb)
                    v.wait_ge(sem("m_dbu"), u * NSG + g + 1)
                    v.wait_ge(sem("m_da"), u * NSG + g + 1)
                    flat = lambda t: t.rearrange("p s n -> p (s n)")
                    v.tensor_tensor_scan(flat(hst[g % 2][:]), flat(da[b][:, SG * g:SG * g + SG]),
                                         flat(dbu[g % 2][:]), 0.0, ALU.mult, ALU.add).then_inc(sem("m_h"), 1)
                    if g == 2 and not last:
                        prep_uc(u + 1, nk, nb)
                    v.wait_ge(sem("m_h"), u * NSG + g + 1)
                    v.wait_ge(sem("m_C"), u * NSG + g + 1)
                    v.tensor_tensor(hc[:, g], hst[g % 2][:], Cv, ALU.mult).then_inc(sem("m_hc"), 1)

            prep_uc(0, 0, 0)
            v_step(0, 0, first=True)
            with v.Fori(0, 2) as i:
                for s in range(1, 5):
                    v_step(i, s)
            for s in range(9, 12):
                v_step(0, s, last=(s == 11))
            gate(UNITS - 1, 1, 1)
            residual(UNITS - 1, 1)
            v.wait_ge(sem("m_res"), UNITS)
            chain(v.tensor_tensor(Zg, Yg, Yg, ALU.mult))
            v.tensor_reduce(small[:, 0:4], Zg, AX.X, ALU.add).then_inc(sem("n_sum"), 1)
            v.wait_ge(sem("n_rstd"), 1)
            for g in range(NG):
                v.scalar_tensor_tensor(Zg[:, g], Yg[:, g], small[:, 8 + g:9 + g], ROWS.of(rowt, "normf"),
                                       ALU.mult, ALU.mult).then_inc(sem("n_out"), 1)
            v.wait_ge(sem("n_out"), NG)
            chain(v.tensor_tensor(Xg, Xg, Zg, ALU.add))

            ln(6, Xg, Yg)
            v.wait_ge(sem("y_T"), 1)
            chain(v.tensor_reduce(small[:, 15:16], PS[:, 0, 0:N], AX.X, ALU.add))
            v.tensor_scalar(small[:, 16:17], small[:, 15:16], 1.0 / N, None, ALU.mult).then_inc(sem("y_mean"), 1)
            apart(PS[:, 0, 0:N], "y_Ts")
            lg, pr, wts, msk = (small[:, 32 + 16 * t:48 + 16 * t] for t in range(4))
            sc2, gt2, eq2 = small[:, 96:98], small[:, 128:256], small[:, 256:384]
            load, br = small[:, 100:108], ROWS.of(rowt, "br3")
            v.wait_ge(sem("y_logit"), 1)
            chain(v.tensor_tensor(per(lg, B), per(PS[:, 1, 0:B * NE], B),
                                  br.unsqueeze(1).to_broadcast([P, B, NE]), ALU.add))
            softmax_shift(lg, lg, sc2, B)
            v.sem_inc(sem("y_shift"), 1)
            v.wait_ge(sem("y_exp"), 1)
            chain(v.tensor_reduce(sc2, per(pr, B), AX.X, ALU.add))
            chain(v.reciprocal(sc2, sc2))
            chain(v.tensor_tensor(per(pr, B), per(pr, B), over(sc2, B), ALU.mult))
            chain(v.tensor_tensor(load, pr[:, 0:NE], pr[:, NE:2 * NE], ALU.add))
            chain(v.reciprocal(load, load))
            chain(v.tensor_scalar(load, load, CAPACITY / N, 1.0, ALU.mult, ALU.min))
            chain(v.tensor_tensor(per(lg, B), per(pr, B), load.unsqueeze(1).to_broadcast([P, B, NE]), ALU.mult))
            softmax_shift(lg, lg, sc2, B)
            v.sem_inc(sem("y_shift"), 1)
            v.wait_ge(sem("y_exp"), 2)
            chain(v.tensor_reduce(sc2, per(pr, B), AX.X, ALU.add))
            chain(v.reciprocal(sc2, sc2))
            chain(v.tensor_tensor(per(pr, B), per(pr, B), over(sc2, B), ALU.mult))
            softmax_shift(lg, pr, sc2, B)
            v.sem_inc(sem("y_shift"), 1)
            top2(msk, pr, B, gt2, eq2)
            v.wait_ge(sem("y_exp"), 3)
            chain(v.tensor_tensor(wts, wts, msk, ALU.mult))
            chain(v.tensor_reduce(sc2, per(wts, B), AX.X, ALU.add))
            chain(v.reciprocal(sc2, sc2))
            chain(v.tensor_tensor(per(wts, B), per(wts, B), over(sc2, B), ALU.mult))
            w2y = W5.of(w5t, "w2").rearrange("p (e c) -> p e c", e=NE)
            for b in range(B):
                v.tensor_tensor(w2w[:, b], w2y, wts[:, b * NE:(b + 1) * NE].unsqueeze(2).to_broadcast([P, NE, D]),
                                ALU.mult).then_inc(sem("y_w2w"), 1)
            chain(v.tensor_tensor(per(lg[0:NE], B), per(wts[0:NE], B),
                                  ident[0:NE, 0:NE].unsqueeze(1).to_broadcast([NE, B, NE]), ALU.mult))
            chain(v.tensor_reduce(sc2[0:NE], per(lg[0:NE], B), AX.X, ALU.add))
            chain(v.tensor_tensor(y_b2w.rearrange("p (b c) -> p b c", b=B),
                                  W5.of(w5t, "b2", NE).unsqueeze(1).to_broadcast([NE, B, D]),
                                  sc2[0:NE].unsqueeze(2).to_broadcast([NE, B, D]), ALU.mult))
            v.memset(y_ones, 1.0).then_inc(sem("y_b2w"), 1)
            v.wait_ge(sem("y_y"), 1)
            v.tensor_copy(T2b[:], PS[:, 4, 0:N]).then_inc(sem("y_ys"), 1)
            v.wait_ge(sem("y_out"), 1)
            chain(v.tensor_tensor(Yg, Yg, PS[:, 5, 0:NG * D].rearrange("p (g c) -> p g c", g=NG), ALU.add))
            ln(7, Yg, Zg, "gamma", "beta")
            v.wait_ge(sem("ln_out"), 6)
            v.tensor_tensor(Zg, Zg, Xg, ALU.add).then_inc(sem("result"), 1)

        @block.scalar
        def _(act):
            act.preload_act_table_set("natural_log_exp_and_others")
            copy = lambda dst, src, **kw: act.activation(dst, src, ACT.Copy, **kw)

            def root(j):
                act.wait_ge(sem("ln_aggr"), (j + 1) * NG)
                act.activation(lnv[:, j], mv[:, j, :, 1], ACT.Ln, bias=eps_t[:]).then_inc(sem("ln_log"), 1)
                act.wait_ge(sem("ln_log"), j + 1)
                act.activation(rstd[:, j], lnv[:, j], ACT.Exp, scale=-0.5).then_inc(sem("ln_rstd"), 1)

            act.wait_ge(sem("consts"), 1)
            act.wait_ge(sem("e_proj"), 1)
            copy(proj[:, 0:2].rearrange("p t n -> p (t n)"), PS[:, 1]).then_inc(sem("e_projs"), 1)
            act.wait_ge(sem("e_proj"), 2)
            copy(proj[:, 2:4].rearrange("p t n -> p (t n)"), PS[:, 2]).then_inc(sem("e_projs"), 1)
            for c in range(8):
                act.wait_ge(sem("e_shift"), c + 1)
                act.activation(strip(expd, c), strip(shifted, c), ACT.Exp, scale=8.0 ** -0.5)\
                    .then_inc(sem("e_exp"), 1)
            root(0)
            act.wait_ge(sem("f0_h"), 1)
            act.activation(mlp_hid.rearrange("p b n -> p (b n)"), PS[:, 3], ACT.Relu, bias=W0.of(w0t, "b1"))\
                .then_inc(sem("f0_relu"), 1)
            root(1)
            act.wait_ge(sem("g_var"), 1)
            act.activation(small[:, 6:7], small[:, 5:6], ACT.Ln, bias=eps_t[:]).then_inc(sem("g_log"), 1)
            act.wait_ge(sem("g_log"), 1)
            act.activation(small[:, 7:8], small[:, 6:7], ACT.Exp, scale=-0.5).then_inc(sem("g_rstd"), 1)

            def attention(base):
                n = B * H8
                for i in range(n + 1):
                    if i < n:
                        act.wait_ge(sem("h_max"), base + i + 1)
                        if i >= 2:
                            act.wait_ge(sem("h_t"), base + i - 1)
                        for a in range(2):
                            act.activation(probs[:, i % 2, a], PS[:, i % 2, a * N:(a + 1) * N], ACT.Exp,
                                           bias=rowmax[:, i, a:a + 1], accum_out=rowsum[:, i, a:a + 1])\
                                .then_inc(sem("h_exp"), 1)
                    if i >= 1:
                        act.wait_ge(sem("h_t"), base + i)
                        if i >= 3:
                            act.wait_ge(sem("h_av"), base + i - 2)
                        copy(probsT[:, (i - 1) % 2].rearrange("p a n -> p (a n)"), PS[:, 2 + (i - 1) % 2])\
                            .then_inc(sem("h_pT"), 1)

            attention(0)
            act.wait_ge(sem("h_av"), B * H8)
            copy(opad[:, 2:4].rearrange("p g n -> p (g n)"), PS[:, 5]).then_inc(sem("r_oT"), 1)
            root(2)
            for c in range(4):
                act.wait_ge(sem("a_proj"), c + 1)
                for j in range(2):
                    copy(qz[64 * j:64 * j + 64, c, j].rearrange("p b n -> p (b n)"), PS[64 * j:64 * j + 64, c],
                         scale=D ** -0.5).then_inc(sem("a_q"), 1)
            attention(B * H8)
            act.wait_ge(sem("h_av"), 2 * B * H8)
            for c in range(2, 4):
                copy(oT[:, c].rearrange("p b n -> p (b n)"), PS[:, 4 + c]).then_inc(sem("a_oT"), 1)
            root(3)
            root(4)
            act.wait_ge(sem("x_shift"), 1)
            act.activation(rt(32, 32), rt(0, 32), ACT.Exp).then_inc(sem("x_exp"), 1)
            act.wait_ge(sem("x_b1s"), 1)
            for e in range(2 * NE):
                act.wait_ge(sem("x_h"), e + 1)
                act.activation(hid[:, e].rearrange("p b n -> p (b n)"), PS[:, 4 + e % 4], ACT.Gelu,
                               bias=b1e[:, e:e + 1]).then_inc(sem("x_gelu"), 1)
            for pair in range(4):
                act.wait_ge(sem("x_wbc"), pair + 1)
                if pair >= 2:
                    act.wait_ge(sem("x_yw"), 2 * pair - 3)
                copy(big[:, 14336 + 512 * (pair % 2):14336 + 512 * (pair % 2 + 1)], PS[:, 5 + pair % 2])\
                    .then_inc(sem("x_wide"), 1)
            act.preload_act_table_set("natural_log_exp_and_others")
            root(5)
            act.preload_act_table_set("exp_and_others")

            def prep_norm(u, k, b, ready=None):
                if ready is None:
                    act.wait_ge(sem("m_res"), u + -1)
                else:
                    act.wait_ge(sem(ready[0]), ready[1])
                for a in range(HALF):
                    act.activation(sqs[:, a], Y[:, a, b], ACT.Square, scale=D ** -0.5,
                                   accum_out=ssq[b][:, a:a + 1]).then_inc(sem("m_ssq"), 1)

            def prep_ht(u, k, b):
                act.wait_ge(sem("m_tr"), u + 1)
                for c in range(2):
                    rows_ = slice(64 * c, 64 * c + 64)
                    act.activation(ht[b][rows_, 3 + c:3 + c + N], tr[rows_], ACT.Copy,
                                   scale=WM.of(wmt[k], "norm")[rows_]).then_inc(sem("m_ht"), 1)

            def prep_sig(u, k, b):
                for s, (src, ready) in enumerate(((ups, "m_up"), (zps[b], "m_zp"))):
                    act.wait_ge(sem(ready), u + 1)
                    act.activation(sg[b][:, s], src, ACT.Tanh, scale=0.5, bias=hbias[k][:] if s == 0 else 0.0)\
                        .then_inc(sem("m_tanh"), 1)
                    act.wait_ge(sem("m_tanh"), u * 2 + s + 1)
                    act.activation(sg[b][:, s], sg[b][:, s], ACT.Copy, scale=0.5, bias=0.5).then_inc(sem("m_sig"), 1)
                act.activation(zs[b][:], zps[b], ACT.Copy).then_inc(sem("m_zs"), 1)

            def prep_xd(u, k, b):
                act.wait_ge(sem("m_xd"), u + 1)
                act.activation(xds[b][0:112], xd, ACT.Copy).then_inc(sem("m_xds"), 1)
                act.wait_ge(sem("m_xds"), u + 1)
                act.activation(stack[b][0:96], xds[b][0:96], ACT.Copy).then_inc(sem("m_hi"), 1)

            def prep_softplus(u, k, b):
                act.wait_ge(sem("m_dtp"), u + 1)
                dtb = WM.of(wmt[k], "dtb")
                act.activation(sp_u[b][:], dtp, ACT.Abs, bias=dtb).then_inc(sem("m_abs"), 1)
                act.wait_ge(sem("m_abs"), u + 1)
                act.activation(sp_u[b][:], sp_u[b][:], ACT.Exp, scale=-1.0).then_inc(sem("m_u"), 1)
                act.wait_ge(sem("m_u"), u + 1)
                for q, (kq, bq, _) in enumerate(quadratics()):
                    act.activation(sp_q[b][:, q], sp_u[b][:], ACT.Square, scale=kq, bias=quad_t[:, q:q + 1])\
                        .then_inc(sem("m_q"), 1)
                act.activation(sp_m[b][:], dtp, ACT.Relu, bias=dtb).then_inc(sem("m_relu"), 1)

            def decay(u, k, b, states):
                for n in states:
                    one = act.activation(da[b][:, n, 1:N], dt[b][:, 1:N], ACT.Exp, scale=amat[k][:, n:n + 1])
                    if n % SG == SG - 1:
                        one.then_inc(sem("m_da"), 1)

            def prep_weights(u, k, b):
                if b == 0:
                    act.activation(alog[k][:], WM.of(wmt[k], "alog"), ACT.Exp).then_inc(sem("m_alog"), 1)

            def a_step(i, s, first=False, last=False):
                u = i * 4 + s
                k, b = (s // 2) % 2, s % 2
                nk, nb = ((s + 1) // 2) % 2, (s + 1) % 2
                act.wait_ge(sem("m_dt"), u + 1)
                act.wait_ge(sem("m_a"), i * 2 + s // 2 + 1)
                decay(u, k, b, range(DS if last else SG + 1))
                if not last:
                    if nb == 0:
                        layer_loaded(act, i, s + 1)
                    prep_norm(u + 1, nk, nb, ("ln_norm", 6 * NG) if first else None)
                    decay(u, k, b, range(SG + 1, 2 * SG))
                    prep_weights(u + 1, nk, nb)
                    prep_ht(u + 1, nk, nb)
                    decay(u, k, b, range(2 * SG, DS))
                    prep_sig(u + 1, nk, nb)
                    prep_xd(u + 1, nk, nb)
                    prep_softplus(u + 1, nk, nb)

            act.wait_ge(sem("ld_wm0"), 16)
            prep_weights(0, 0, 0)
            prep_norm(0, 0, 0, ("ln_norm", 6 * NG))
            prep_ht(0, 0, 0)
            prep_sig(0, 0, 0)
            prep_xd(0, 0, 0)
            prep_softplus(0, 0, 0)
            a_step(0, 0, first=True)
            with act.Fori(0, 2) as i:
                for s in range(1, 5):
                    a_step(i, s)
            for s in range(9, 12):
                a_step(0, s, last=(s == 11))

            act.preload_act_table_set("natural_log_exp_and_others")
            act.wait_ge(sem("n_sum"), 1)
            act.activation(small[:, 4:8], small[:, 0:4], ACT.Ln, scale=1.0 / D, bias=eps_t[:])\
                .then_inc(sem("n_log"), 1)
            act.wait_ge(sem("n_log"), 1)
            act.activation(small[:, 8:12], small[:, 4:8], ACT.Exp, scale=-0.5).then_inc(sem("n_rstd"), 1)

            root(6)
            slg, spr, swt = small[:, 32:48], small[:, 48:64], small[:, 64:80]
            for n, dst in enumerate((spr, spr, swt)):
                act.wait_ge(sem("y_shift"), n + 1)
                act.activation(dst, slg, ACT.Exp).then_inc(sem("y_exp"), 1)
            for e in range(NE):
                act.wait_ge(sem("y_h"), e + 1)
                act.activation(hid5[:, e].rearrange("p b n -> p (b n)"), PS[:, y_bank[e]], ACT.Gelu,
                               bias=W5.of(w5t, "b1")[:, e:e + 1]).then_inc(sem("y_gelu"), 1)
            act.preload_act_table_set("natural_log_exp_and_others")
            root(7)

        @block.gpsimd
        def _(pool):
            for q, (_, bq, _) in enumerate(quadratics()):
                pool.memset(quad_t[:, q:q + 1], bq).then_inc(sem("filled"), 1)
            pool.memset(zero_t[:], 0.0).then_inc(sem("filled"), 1)
            pool.memset(half_t[:], 0.5).then_inc(sem("filled"), 1)
            pool.memset(power_t[:], -0.5).then_inc(sem("filled"), 1)
            pool.memset(T2d[:], 0.0).then_inc(sem("filled"), 1)
            pool.memset(eps_t[:], EPS).then_inc(sem("consts"), 1)
            pool.wait_ge(sem("e_projs"), 2)
            for c in range(8):
                l = proj[:, 2].rearrange("p (x a) -> p a x", a=GRID)[:, :, 2 * c:2 * c + 2]
                r = proj[:, 3].rearrange("p (a y) -> p a y", a=GRID)
                pool.tensor_tensor(strip(lvrv, c).rearrange("p a (x y) -> p a x y", y=GRID),
                                   l.unsqueeze(3).to_broadcast([P, GRID, 2, GRID]),
                                   r.unsqueeze(2).to_broadcast([P, GRID, 2, GRID]), ALU.mult)\
                    .then_inc(sem("e_lvrv"), 1)
            pool.wait_ge(sem("e_exp"), 8)
            pool.wait_ge(sem("e_lvrv"), 8)
            pool.tensor_tensor(half_of(shifted, 1), half_of(expd, 1), half_of(lvrv, 1), ALU.mult).then_inc(sem("e_ev"), 1)
            for b in range(B):
                pool.memset(ht[b][:], 0.0).then_inc(sem("filled"), 1)
            pool.memset(qz, 0.0).then_inc(sem("filled"), 1)
            pool.wait_ge(sem("ld_const"), 16)
            pool.tensor_copy(pick_b[:], CONST.of(cst, "pick")).then_inc(sem("filled"), 1)
            pool.wait_ge(sem("e_o"), 1)
            pool.memset(vpad, 0.0).then_inc(sem("r_vs"), 1)
            pool.wait_ge(sem("r_rope"), 1)
            for i in range(B * H8):
                pool.tensor_scalar(qm[:, i], roped[:, 0], head_mask(i), None, ALU.mult).then_inc(sem("r_qm"), 1)
            pool.wait_ge(sem("ld_w3"), 16)
            for e in range(NE):
                pool.tensor_scalar(w1g[:, e * HID2:(e + 1) * HID2], W3.of(w3t, "w1")[:, e * HID2:(e + 1) * HID2],
                                   W3.of(w3t, "g")[:, e:e + 1], None, ALU.mult).then_inc(sem("x_w1g"), 1)

            def prep_weights(i, s, k):
                layer_loaded(pool, i, s)
                pool.tensor_tensor(hbias[k][:], WM.of(wmt[k], "cb"), half_t[:], ALU.mult).then_inc(sem("m_hb"), 1)
                pool.tensor_tensor(wcv[k][:].rearrange("p (t n) -> p t n", t=2),
                                   WM.of(wmt[k], "inu").unsqueeze(1).to_broadcast([P, 2, P]),
                                   WM.of(wmt[k], "cw").rearrange("p (t n) -> p t n", t=2), ALU.mult)\
                    .then_inc(sem("m_wc"), 1)

            def prep_rates(i, s, k):
                pool.wait_ge(sem("m_alog"), i * 2 + s // 2 + 1)
                pool.tensor_tensor(amat[k][:], zero_t[:].to_broadcast([P, DS]), alog[k][:], ALU.subtract)\
                    .then_inc(sem("m_a"), 1)
                pool.tensor_tensor(dmat[k][:], ident, WM.of(wmt[k], "d").to_broadcast([P, P]), ALU.mult)\
                    .then_inc(sem("m_d"), 1)

            def prep_scale(u, b):
                pool.wait_ge(sem("m_ssq"), u * 2 + 2)
                pool.tensor_tensor(msq[b][:], ssq[b][:], eps_t[:].to_broadcast([P, 2]), ALU.add)\
                    .then_inc(sem("m_msq"), 1)
                pool.wait_ge(sem("m_msq"), u + 1)
                pool.tensor_tensor(rms[b][:], msq[b][:], power_t[:].to_broadcast([P, 2]), ALU.pow)\
                    .then_inc(sem("m_rms"), 1)
                pool.wait_ge(sem("m_rms"), u + 1)
                sh = [P, HALF, 2, D]
                pool.tensor_tensor(hs2[b][:].rearrange("p a (c e) -> p a c e", c=2),
                                   Y[:, :, b].unsqueeze(2).to_broadcast(sh),
                                   rms[b][:].unsqueeze(2).unsqueeze(3).to_broadcast(sh), ALU.mult)\
                    .then_inc(sem("m_hs"), 1)

            def prep_gz(u, b):
                pool.wait_ge(sem("m_stack"), u + 1)
                pool.wait_ge(sem("m_zs"), u + 1)
                pool.tensor_tensor(gz[b][:], zs[b][:], sg[b][:, 1], ALU.mult).then_inc(sem("m_gz"), 1)

            def prep_stack(u, b):
                pool.wait_ge(sem("m_hi"), u + 1)
                pool.wait_ge(sem("m_xds"), u + 1)
                pool.tensor_tensor(rest[:], xds[b][0:96], stack[b][0:96], ALU.subtract).then_inc(sem("m_split"), 1)
                pool.wait_ge(sem("m_split"), u * 3 + 1)
                pool.tensor_tensor(stack[b][32:64], rest[32:64], zero_t[32:64].to_broadcast([32, N]),
                                   ALU.add).then_inc(sem("m_split"), 1)
                pool.wait_ge(sem("m_split"), u * 3 + 2)
                pool.tensor_tensor(stack[b][64:96], rest[64:96], zero_t[64:96].to_broadcast([32, N]),
                                   ALU.add).then_inc(sem("m_split"), 1)
                pool.wait_ge(sem("m_split"), u * 3 + 3)
                pool.tensor_tensor(stack[b][64:96], rest[64:96], stack[b][64:96], ALU.subtract)\
                    .then_inc(sem("m_stack"), 1)

            def pair_sum(u):
                pool.wait_ge(sem("m_hc"), u * NSG + 2)
                pool.tensor_tensor(hc[:, 0], hc[:, 0], hc[:, 1], ALU.add).then_inc(sem("m_pair"), 1)

            def p_prep(i, s, pair=True):
                u, k, b = i * 4 + s, (s // 2) % 2, s % 2
                if b == 0:
                    prep_weights(i, s, k)
                prep_scale(u, b)
                if b == 0:
                    prep_rates(i, s, k)
                if pair:
                    pair_sum(u + -1)
                prep_stack(u, b)
                prep_gz(u, b)

            pool.wait_ge(sem("x_out"), 1)
            for b in range(B):
                pool.memset(da[b][:, :, 0:1], 0.0).then_inc(sem("filled"), 1)
            p_prep(0, 0, pair=False)
            p_prep(0, 1)
            with pool.Fori(0, 2) as i:
                for s in range(2, 6):
                    p_prep(i, s)
            for s in range(10, 12):
                p_prep(0, s)
            pair_sum(UNITS - 1)


def constants():
    c = np.zeros((P, CONST.size), np.float32)
    part = lambda name, rows=P: CONST.of(c, name, rows)
    r = np.arange(P)
    part("ident")[:] = np.eye(P)
    part("heads")[:] = r[:, None] // 8 == r[None, :] // 8
    part("pairs")[:] = 0.5 * (r[:, None] // 2 == r[None, :] // 2)
    inv = 1.0 / 10000.0 ** (np.arange(0, 8, 2) / 8.0)
    ang = np.arange(N)[None, :] * inv[r % 4][:, None]
    cos, sin = np.cos(ang), np.sin(ang) * np.where(r % 8 < 4, -1.0, 1.0)[:, None]
    scale = 8.0 ** -0.5
    part("rope")[:] = np.concatenate([cos * scale, sin * scale, cos, sin], axis=1)
    part("fold")[:] = np.concatenate([np.eye(D), np.eye(D)])
    e = np.zeros((NE, 4, P), np.float32)
    for n in range(NE):
        e[n, n // 2, 64 * (n % 2):64 * (n % 2) + 64] = 1.0
    part("experts", NE)[:] = e.reshape(NE, -1)
    part("before")[:] = (np.arange(NE)[None, :] < np.arange(NE)[:, None]).reshape(-1).astype(np.float32)
    part("pick")[:] = (r[:, None] % 32 == np.arange(32)[None, :]) * (r[:, None] < 96)
    return c


def twice(w):
    return np.concatenate([w, w], axis=0)


def diagonal(w):
    z = np.zeros_like(w)
    return np.concatenate([np.concatenate([w, z], 1), np.concatenate([z, w], 1)], 0)


def packed(columns, parts):
    out = np.zeros((P, columns.size), np.float32)
    for name, value in parts.items():
        value = np.asarray(value, np.float32)
        columns.of(out, name, value.shape[0])[:] = value
    return out


def laid_out(i):
    col = lambda a: np.asarray(a).reshape(-1, 1)
    w0 = packed(W0, {**{n: diagonal(i["L0_conv_W_" + n]) for n in ("lk", "lv", "rk", "rv", "out")},
                     "w1": twice(i["L0_conv_W1"]), "w2": i["L0_conv_W2"], "b1": col(i["L0_conv_b1"])})
    swap = np.arange(D) // 8 * 8 + (np.arange(D) + 4) % 8
    wo = np.asarray(i["L1_conv_Wo"]).T
    wo_pad = np.zeros((P, 2, D), np.float32)
    for h in range(H8):
        wo_pad[32 * (h % 4):32 * (h % 4) + 8, h // 4] = wo[8 * h:8 * h + 8]
    wq, wk, wv = (np.asarray(i["L1_conv_W" + n]).T for n in "qkv")
    qb = np.asarray(i["L1_conv_q_bias"])
    w1 = packed(W1, {"q": diagonal(wq), "qs": diagonal(wq[:, swap]), "k": diagonal(wk), "ks": diagonal(wk[:, swap]),
                     "v": diagonal(wv), "o": wo_pad.reshape(P, -1), "qb": twice(col(qb)),
                     "qsb": twice(col(qb[swap]))})
    w2 = packed(W2, {"q": twice(i["L2_attn_Wq"]), "k": twice(i["L2_attn_Wk"]), "v": twice(i["L2_attn_Wv"]),
                     "u": np.asarray(i["L2_attn_Wu"]).reshape(4, P, D).transpose(1, 0, 2).reshape(P, -1)})
    flat = lambda w: np.asarray(w).transpose(1, 0, 2).reshape(np.asarray(w).shape[1], -1)
    w3 = packed(W3, {"wr": twice(i["L2_ffn_Wr"]), "w1": twice(flat(i["L2_ffn_W1"])),
                     "w2": flat(np.asarray(i["L2_ffn_W2"]).reshape(2 * NE, P, D)),
                     "b1": np.asarray(i["L2_ffn_b1"]).reshape(2 * NE, P).T,
                     "g": twice(np.asarray(i["L2_ffn_ln_g"]).T), "b": twice(np.asarray(i["L2_ffn_ln_b"]).T),
                     "b2": i["L2_ffn_b2"]})
    w5 = packed(W5, {"wr": diagonal(np.asarray(i["L3_ffn_Wr"])), "w1": twice(flat(i["L3_ffn_W1"])),
                     "w2": flat(i["L3_ffn_W2"]), "b1": np.asarray(i["L3_ffn_b1"]).T, "b2": i["L3_ffn_b2"]})
    m = {n[8:]: np.asarray(v) for n, v in i.items() if n.startswith("L3_attn_")}
    layers = []
    for n in range(NL):
        taps = m["conv_w"][n].T
        cw = np.concatenate([np.broadcast_to(taps[[3, 1]].reshape(1, -1), (D, 2 * P)),
                             np.broadcast_to(taps[[2, 0]].reshape(1, -1), (D, 2 * P))])
        xp = m["x_proj_w"][n]
        dtw = np.zeros((P, P), np.float32)
        dtw[96:112] = m["dt_proj_w"][n]
        layers.append(packed(WM, {
            "inu": twice(m["in_proj_w"][n][:, :DI]), "cw": cw, "inz": m["in_proj_w"][n][:, DI:],
            "xp": np.concatenate([xp[:, RANK:]] * 3 + [xp[:, :RANK]], axis=1), "dtw": dtw,
            "out": m["out_proj_w"][n], "alog": m["A_log"][n], "cb": col(m["conv_b"][n]),
            "dtb": col(m["dt_proj_b"][n]), "d": col(m["D"][n]), "norm": twice(col(m["norm_w"][n]))}))
    rows = np.concatenate([np.asarray(i[n]).reshape(-1) for n in (
        "L0_conv_ln_agg_g", "L0_conv_ln_agg_b", "L0_conv_b2", "L0_conv_ln2_g", "L0_conv_ln2_b", "L1_conv_v_bias",
        "L1_conv_bo", "L2_attn_bu", "L3_attn_norm_f_w", "L3_ffn_gamma", "L3_ffn_beta", "L2_ffn_br",
        "L3_ffn_br")])
    return {"x": np.ascontiguousarray(i["x"]), "const": constants(), "w0": w0, "w1": w1, "w2": w2, "w3": w3,
            "w5": w5, "wm": np.stack(layers), "rows": rows}


def kernel(**inputs):
    import concourse.bacc as bacc
    from concourse.bass_utils import run_bass_kernel_spmd

    arrays = laid_out({n: np.asarray(v) for n, v in inputs.items()})
    nc = bacc.Bacc("TRN2", target_bir_lowering=False, num_devices=1)
    args = [nc.dram_tensor("in_" + n, a.shape, F32, kind="ExternalInput").ap() for n, a in arrays.items()]
    out = nc.dram_tensor("out", (B, GRID, GRID, D), F32, kind="ExternalOutput").ap()
    hybrid(nc, *args, out)
    r = run_bass_kernel_spmd(nc, [{"in_" + n: a for n, a in arrays.items()}], core_ids=[0])
    return r.results[0]["out"]
```
